# Optimizing a Trainium2 kernel written in Bass

```python
import numpy as np
import jax
import jax.numpy as jnp

def _softmax(x, axis=-1):
    return jax.nn.softmax(x, axis=axis)

def _gelu(x):
    return jax.nn.gelu(x, approximate=True)

def _silu(x):
    return jax.nn.silu(x)

def _sigmoid(x):
    return jax.nn.sigmoid(x)

def _layernorm(x, axis=-1, eps=1e-05):
    m = jnp.mean(x, axis=axis, keepdims=True)
    v = jnp.var(x, axis=axis, keepdims=True)
    return (x - m) / jnp.sqrt(v + eps)

def _scatter_add(tgt, idx, src, axis=0):
    return tgt.at[idx].add(src)

def _segment_sum(src, seg, n):
    return jax.ops.segment_sum(src, seg, n)
kernel_name = 'mk_prb_d1_jaxref_r4_8a2246'

def setup_inputs(seed: int=0):
    np.random.seed(seed)
    _w = jnp.asarray

    def _L0_attn_setup():
        import jax, jax.numpy as jnp
        import numpy as np
        import math
        EMBED_DIM = 256
        NUM_HEADS = 16
        HEAD_DIM = EMBED_DIM // NUM_HEADS
        MAX_POS = 128
        SPARSE_TOPK = 32
        B, T = (8, 128)
        key = jax.random.key(seed)
        ks = jax.random.split(key, 12)
        s = 1.0 / math.sqrt(EMBED_DIM)
        inp = {'x': jax.random.normal(ks[0], (B, T, EMBED_DIM), dtype=jnp.float32), 'Wq': jax.random.uniform(ks[1], (EMBED_DIM, EMBED_DIM), jnp.float32, -s, s), 'bq': jax.random.uniform(ks[2], (EMBED_DIM,), jnp.float32, -s, s), 'Wk': jax.random.uniform(ks[3], (EMBED_DIM, EMBED_DIM), jnp.float32, -s, s), 'bk': jax.random.uniform(ks[4], (EMBED_DIM,), jnp.float32, -s, s), 'Wv': jax.random.uniform(ks[5], (EMBED_DIM, EMBED_DIM), jnp.float32, -s, s), 'bv': jax.random.uniform(ks[6], (EMBED_DIM,), jnp.float32, -s, s), 'Wo': jax.random.uniform(ks[7], (EMBED_DIM, EMBED_DIM), jnp.float32, -s, s), 'bo': jax.random.uniform(ks[8], (EMBED_DIM,), jnp.float32, -s, s), 'head_gates': jnp.ones((NUM_HEADS,), dtype=jnp.float32), 'rel_bias': 0.02 * jax.random.normal(ks[9], (2 * MAX_POS - 1, NUM_HEADS), dtype=jnp.float32)}
        return inp
    _L0_attn_in = _L0_attn_setup()

    def _L0_ffn_setup():
        import jax, jax.numpy as jnp
        import numpy as np
        import math
        D_IN = 256
        FEATURES = (1024, 1024, 256)
        BATCH, SEQ = (8, 512)

        def _conn_dense(kernel_bool, x):
            w = jnp.where(kernel_bool, jnp.float32(1.0), jnp.float32(-1.0))
            return x @ w
        key = jax.random.key(seed)
        kx, kk0, kk1, kk2 = jax.random.split(key, 4)
        x = jax.random.normal(kx, (BATCH, SEQ, D_IN), dtype=jnp.float32)
        k0 = jax.random.randint(kk0, (2 * D_IN, FEATURES[0]), 0, 2).astype(jnp.bool_)
        k1 = jax.random.randint(kk1, (FEATURES[0], FEATURES[1]), 0, 2).astype(jnp.bool_)
        k2 = jax.random.randint(kk2, (FEATURES[1], FEATURES[2]), 0, 2).astype(jnp.bool_)
        s0 = jnp.asarray(1.0 / math.sqrt(2 * D_IN), dtype=jnp.float32)
        s1 = jnp.asarray(1.0 / math.sqrt(FEATURES[0]), dtype=jnp.float32)
        s2 = jnp.asarray(1.0 / math.sqrt(FEATURES[1]), dtype=jnp.float32)
        return {'x': x, 'k0': k0, 'k1': k1, 'k2': k2, 's0': s0, 's1': s1, 's2': s2}
    _L0_ffn_in = _L0_ffn_setup()
    _d = {'L0_attn_x': _L0_attn_in['x'], 'L0_attn_Wq': _L0_attn_in['Wq'], 'L0_attn_bq': _L0_attn_in['bq'], 'L0_attn_Wk': _L0_attn_in['Wk'], 'L0_attn_bk': _L0_attn_in['bk'], 'L0_attn_Wv': _L0_attn_in['Wv'], 'L0_attn_bv': _L0_attn_in['bv'], 'L0_attn_Wo': _L0_attn_in['Wo'], 'L0_attn_bo': _L0_attn_in['bo'], 'L0_attn_head_gates': _L0_attn_in['head_gates'], 'L0_attn_rel_bias': _L0_attn_in['rel_bias'], 'L0_ffn_k0': _L0_ffn_in['k0'], 'L0_ffn_k1': _L0_ffn_in['k1'], 'L0_ffn_k2': _L0_ffn_in['k2'], 'L0_ffn_s0': _L0_ffn_in['s0'], 'L0_ffn_s1': _L0_ffn_in['s1'], 'L0_ffn_s2': _L0_ffn_in['s2']}
    _x0 = _d['L0_attn_x']
    _d['L0_attn_x'] = jax.random.normal(jax.random.fold_in(jax.random.key(seed), 1), (8, 1024, 256), dtype=_x0.dtype)
    del _x0
    return _d

def reference(L0_attn_x, L0_attn_Wq, L0_attn_bq, L0_attn_Wk, L0_attn_bk, L0_attn_Wv, L0_attn_bv, L0_attn_Wo, L0_attn_bo, L0_attn_head_gates, L0_attn_rel_bias, L0_ffn_k0, L0_ffn_k1, L0_ffn_k2, L0_ffn_s0, L0_ffn_s1, L0_ffn_s2):

    def _L0_attn_ref(x, Wq, bq, Wk, bk, Wv, bv, Wo, bo, head_gates, rel_bias):
        import jax, jax.numpy as jnp
        import numpy as np
        import math
        EMBED_DIM = 256
        NUM_HEADS = 16
        HEAD_DIM = EMBED_DIM // NUM_HEADS
        MAX_POS = 128
        SPARSE_TOPK = 32
        B, T = (8, 128)
        Bb, Tt, C = x.shape
        H, D = (NUM_HEADS, HEAD_DIM)
        q = (x @ Wq.T + bq).reshape(Bb, Tt, H, D).transpose(0, 2, 1, 3)
        k = (x @ Wk.T + bk).reshape(Bb, Tt, H, D).transpose(0, 2, 1, 3)
        v = (x @ Wv.T + bv).reshape(Bb, Tt, H, D).transpose(0, 2, 1, 3)
        scores = jnp.einsum('bhqd,bhkd->bhqk', q, k) / math.sqrt(D)
        idx = jnp.arange(Tt)
        rel = idx[None, :] - idx[:, None] + (MAX_POS - 1)
        pos_bias = rel_bias[rel].transpose(2, 0, 1)[None]
        scores = scores + pos_bias
        if SPARSE_TOPK > 0:
            topk_vals, _ = jax.lax.top_k(scores, SPARSE_TOPK)
            thresh = topk_vals[..., -1:]
            scores = jnp.where(scores >= thresh, scores, -jnp.inf)
        weights = jax.nn.softmax(scores, axis=-1)
        gated = weights * head_gates[None, :, None, None]
        attn_out = jnp.einsum('bhqk,bhkd->bhqd', gated, v)
        attn_out = attn_out.transpose(0, 2, 1, 3).reshape(Bb, Tt, C)
        return attn_out @ Wo.T + bo

    def _L0_ffn_ref(x, k0, k1, k2, s0, s1, s2):
        import jax, jax.numpy as jnp
        import numpy as np
        import math
        D_IN = 256
        FEATURES = (1024, 1024, 256)
        BATCH, SEQ = (8, 512)

        def _conn_dense(kernel_bool, x):
            w = jnp.where(kernel_bool, jnp.float32(1.0), jnp.float32(-1.0))
            return x @ w
        h = jnp.concatenate([x, -x], axis=-1)
        h = s0 * _conn_dense(k0, h)
        h = jax.nn.relu(h) * 2
        h = s1 * _conn_dense(k1, h)
        h = jax.nn.relu(h) * 2
        h = s2 * _conn_dense(k2, h)
        return h
    x = L0_attn_x
    xn = _layernorm(x, axis=-1)
    x = x + _L0_attn_ref(xn, L0_attn_Wq, L0_attn_bq, L0_attn_Wk, L0_attn_bk, L0_attn_Wv, L0_attn_bv, L0_attn_Wo, L0_attn_bo, L0_attn_head_gates, L0_attn_rel_bias) + _L0_ffn_ref(xn, L0_ffn_k0, L0_ffn_k1, L0_ffn_k2, L0_ffn_s0, L0_ffn_s1, L0_ffn_s2)
    return x

_drawn_inputs = setup_inputs


def setup_inputs(seed=0):
    import zlib

    import numpy as np

    out = dict(_drawn_inputs(seed))
    spreads = {'L0_attn_head_gates': (1.0, 0.6)}
    factors = {'L0_attn_bq': 26.107,
     'L0_attn_bk': 200.0,
     'L0_attn_bv': 6.925,
     'L0_attn_bo': 3.562,
     'L0_attn_rel_bias': 99.78,
     'L0_attn_Wq': 3.508}
    for name, (base, spread) in spreads.items():
        noise = np.random.default_rng([zlib.crc32(name.encode()), seed]).standard_normal(out[name].shape)
        drawn = base * np.exp(spread * noise) if base else spread * noise
        out[name] = jnp.asarray(drawn.astype(out[name].dtype))
    for name, factor in factors.items():
        out[name] = (out[name] * factor).astype(out[name].dtype)
    return out
```

```python
from contextlib import ExitStack

import concourse.bass as bass
from concourse import mybir

F32 = mybir.dt.float32
BF16 = mybir.dt.bfloat16
U8 = mybir.dt.uint8
ALU = mybir.AluOpType
ACT = mybir.ActivationFunctionType

P = 128
H, D = 16, 16
TOPK = 32
MAXPOS = 128
EPS = 1e-5
NEG = -3.0e38
HQ = 4
PD = 32
BAND = 5
QROWS = 96
PAIRS = [(0, 0), (0, 1), (1, 0), (1, 1), (0, 2), (2, 0)]


def holder(tick):
    def hold(eng, sem, value):
        eng.wait_ge(sem, value)
        if not isinstance(value, int):
            eng.sem_inc(tick, 1)
    return hold


def attention_ffn_kernel(nc, x, Wq, bq, Wk, bk, Wv, bv, Wo, bo, gates, rel, k0, k1, k2, s0, s1, s2, out):
    B, T, C = x.shape
    F0, F1 = k0.shape[1], k1.shape[1]
    KB = T // P
    NCH = B * 2
    CH = T // 2
    CT = CH // P
    CK = C // P
    QUADS = H // HQ
    TILES = KB * HQ
    BW = BAND * P
    FV = T // 2 + 2 * P
    assert CK == 2 and H * D == C and F0 == 1024 and F1 == 1024

    fvec = nc.dram_tensor("fvec", [H, FV], F32).ap()
    toep = nc.dram_tensor("toep", [H, P, 3 * BW], BF16).ap()
    q_parts = nc.dram_tensor("q_parts", [B, 3, C, T], BF16).ap()
    k_parts = nc.dram_tensor("k_parts", [B, 3, C, T], BF16).ap()
    v_pad = nc.dram_tensor("v_pad", [B, P, H, KB, PD], F32).ap()
    far_q = nc.dram_tensor("far_q", [3, KB, H, T], BF16).ap()
    block_of_key = nc.dram_tensor("block_of_key", [KB, T], BF16).ap()
    resid = nc.dram_tensor("resid", [B, T, C], F32).ap()

    nc.disable_value_cache = True
    with ExitStack() as whole:
        def tensors(ctx):
            return (lambda n, s, d=F32: ctx.enter_context(nc.sbuf_tensor(n, s, d)),
                    lambda n, s, d=F32: ctx.enter_context(nc.psum_tensor(n, s, d)),
                    lambda n: ctx.enter_context(nc.semaphore(n)))

        sb, _, _ = tensors(whole)
        ident = sb("ident", [P, P])
        flip = sb("flip", [P, P], BF16)
        woT = sb("woT", [P, QUADS, C])
        with ExitStack() as early:
            sbe, _, _ = tensors(early)
            wT = sbe("wT", [P, 3, CK, C])
            w0 = sbe("w0", [P, CK, F0])
            w1 = sbe("w1", [P, F0 // P, F1])
            w2 = sbe("w2", [P, F1 // P, C])
            bqk = sbe("bqk", [P, 2, CK])
            bvB = sbe("bvB", [P, C])
            boB = sbe("boB", [P, C])
            scales = sbe("scales", [P, 3])
            with ExitStack() as ctx:
                setup(nc, tensors(ctx), locals())
            with ExitStack() as ctx:
                project(nc, tensors(ctx), locals())
        with ExitStack() as ctx:
            attend(nc, tensors(ctx), locals())


def setup(nc, makers, g):
    sb, psum, sem = makers
    x, Wq, bq, Wk, bk, Wv, bv, Wo, bo = (g[n] for n in ("x", "Wq", "bq", "Wk", "bk", "Wv", "bv", "Wo", "bo"))
    gates, rel, k0, k1, k2, s0, s1, s2 = (g[n] for n in ("gates", "rel", "k0", "k1", "k2", "s0", "s1", "s2"))
    ident, flip, woT, wT, w0, w1, w2 = (g[n] for n in ("ident", "flip", "woT", "wT", "w0", "w1", "w2"))
    bqk, bvB, boB, scales = (g[n] for n in ("bqk", "bvB", "boB", "scales"))
    fvec, toep, far_q, block_of_key = (g[n] for n in ("fvec", "toep", "far_q", "block_of_key"))
    C, T, KB, CK, QUADS, BW, FV = (g[n] for n in ("C", "T", "KB", "CK", "QUADS", "BW", "FV"))
    NR = 2 * MAXPOS - 1

    w_nat = sb("w_nat", [P, 4, CK, C])
    kb0 = sb("kb0", [P, 2 * CK, 1024], U8)
    kb1 = sb("kb1", [P, 8, 1024], U8)
    kb2 = sb("kb2", [P, 8, C], U8)
    gateB = sb("gateB", [P, H])
    wo_pad = sb("wo_pad", [P, CK, H, PD])
    relT = sb("relT", [H, NR])
    fv = sb("fv", [H, FV])
    far = sb("far", [KB, 2, H])
    m_lo = sb("m_lo", [KB, KB])
    m_hi = sb("m_hi", [KB, KB])
    f_a = sb("f_a", [KB, H, KB])
    f_b = sb("f_b", [KB, H, KB])
    f_part = sb("f_part", [KB, 3, H, KB], BF16)
    f_wide = sb("f_wide", [KB, H, KB, P], BF16)
    onehot = sb("onehot", [KB, KB, P], BF16)
    t_f = sb("t_f", [P, 4, BW])
    t_part = sb("t_part", [P, 4, 3, BW], BF16)
    ps_w = psum("ps_w", [P, 3, CK, C])
    ps_o = psum("ps_o", [P, QUADS, C])

    loaded = sem("loaded")
    rel_loaded = sem("rel_loaded")
    table_done = sem("table_done")
    table_out = sem("table_out")
    band_in = sem("band_in")
    band_done = sem("band_done")
    band_out = sem("band_out")
    far_done = sem("far_done")
    far_out = sem("far_out")
    ident_done = sem("ident_done")
    pool_step = sem("pool_step")
    dve_step = sem("dve_step")
    wo_ready = sem("wo_ready")
    turned = sem("turned")
    LOADS = 15 * 16

    with nc.Block() as block:

        @block.sync
        def _(sp):
            with nc.allow_non_contiguous_dma("short vectors"):
                sp.dma_start(relT[:, :], rel.rearrange("r h -> h r")).then_inc(rel_loaded, 16)
                sp.dma_start(far[:, 0, :], rel[0, :].partition_broadcast(KB)).then_inc(rel_loaded, 16)
                sp.dma_start(far[:, 1, :], rel[NR - 1, :].partition_broadcast(KB)).then_inc(rel_loaded, 16)
                for n, w in enumerate((Wq, Wk, Wv, Wo)):
                    sp.dma_start(w_nat[:, n, :, :], w.rearrange("(o p) i -> p o i", p=P)).then_inc(loaded, 16)
                for dst, src in ((kb0, k0), (kb1, k1), (kb2, k2)):
                    sp.dma_start(dst[:, :, :], src.rearrange("(k p) n -> p k n", p=P)).then_inc(loaded, 16)
                for n, b in enumerate((bq, bk)):
                    sp.dma_start(bqk[:, n, :], b.rearrange("(m p) -> p m", p=P)).then_inc(loaded, 16)
                sp.dma_start(bvB[:, :], bv.partition_broadcast(P)).then_inc(loaded, 16)
                sp.dma_start(boB[:, :], bo.partition_broadcast(P)).then_inc(loaded, 16)
                sp.dma_start(gateB[:, :], gates.partition_broadcast(P)).then_inc(loaded, 16)
                for n, s in enumerate((s0, s1, s2)):
                    sp.dma_start(scales[:, n:n + 1], s.partition_broadcast(P)).then_inc(loaded, 16)
            sp.wait_ge(table_done, 1)
            sp.dma_start(fvec, fv[:, :]).then_inc(table_out, 16)
            sp.wait_ge(table_out, 16)
            for n in range(H // 4):
                if n:
                    sp.wait_ge(band_done, n)
                for h in range(4 * n, 4 * n + 4):
                    src = bass.AP(tensor=fvec.tensor, offset=h * FV, ap=[[1, P], [1, BW]])
                    sp.dma_start(t_f[:, h % 4, :], src).then_inc(band_in, 16)
                sp.wait_ge(band_done, n + 1)
                sp.dma_start(toep[4 * n:4 * n + 4].rearrange("h p c -> p h c"),
                             t_part[:, :, :, :].rearrange("p h s c -> p h (s c)")).then_inc(band_out, 16)
            sp.wait_ge(ident_done, 3)
            sp.dma_start(block_of_key, onehot[:, :, :].rearrange("r b c -> r (b c)")).then_inc(far_out, 16)
            for s in range(3):
                sp.wait_ge(far_done, s + 1)
                sp.dma_start(far_q[s], f_wide[:, :, :, :].rearrange("r h i c -> r h (i c)")).then_inc(far_out, 16)
            sp.wait_ge(far_out, 64)
            sp.wait_ge(band_out, 16 * (H // 4))

        @block.gpsimd
        def _(pool):
            def link(ins, count=[0]):
                count[0] += 1
                ins.then_inc(pool_step, 1)
                pool.wait_ge(pool_step, count[0])

            link(pool.memset(ident[:, :], 0.0))
            pool.affine_select(out=ident[:, :], in_=ident[:, :], compare_op=ALU.not_equal, fill=1.0,
                               base=0, pattern=[[-1, P]], channel_multiplier=1).then_inc(ident_done, 1)
            link(pool.memset(flip[:, :], 0.0))
            pool.affine_select(out=flip[:, :], in_=flip[:, :], compare_op=ALU.not_equal, fill=1.0,
                               base=1 - P, pattern=[[1, P]], channel_multiplier=1)
            link(pool.memset(onehot[:, :, :], 1.0))
            pool.affine_select(out=onehot[:, :, :], in_=onehot[:, :, :], compare_op=ALU.is_equal, fill=0.0,
                               base=0, pattern=[[-1, KB], [0, P]], channel_multiplier=1).then_inc(ident_done, 1)
            link(pool.memset(m_lo[:, :], 1.0))
            link(pool.memset(m_hi[:, :], 1.0))
            link(pool.affine_select(out=m_lo[:, :], in_=m_lo[:, :], compare_op=ALU.is_ge, fill=0.0,
                                    base=-4, pattern=[[1, KB]], channel_multiplier=-1))
            pool.affine_select(out=m_hi[:, :], in_=m_hi[:, :], compare_op=ALU.is_ge, fill=0.0,
                               base=-2, pattern=[[-1, KB]], channel_multiplier=1).then_inc(ident_done, 1)

        @block.vector
        def _(dve):
            def link(ins, count=[0]):
                count[0] += 1
                ins.then_inc(dve_step, 1)
                dve.wait_ge(dve_step, count[0])

            def parts(dst, src):
                link(dve.tensor_copy(dst(0), src))
                link(dve.tensor_tensor(src, src, dst(0), ALU.subtract))
                link(dve.tensor_copy(dst(1), src))
                link(dve.tensor_tensor(src, src, dst(1), ALU.subtract))
                return dve.tensor_copy(dst(2), src)

            dve.wait_ge(rel_loaded, 48)
            a = FV - 1 - P - 2 * NR
            dve.tensor_copy(fv[:, 0:a], relT[:, 0:1].broadcast_to([H, a]))
            dve.tensor_copy(fv[:, a:a + NR], relT[:, :])
            dve.tensor_copy(fv[:, a + NR:a + 2 * NR], relT[:, :])
            dve.tensor_copy(fv[:, a + 2 * NR:FV], relT[:, NR - 1:NR].broadcast_to([H, FV - a - 2 * NR]))\
               .then_inc(table_done, 1)
            dve.wait_ge(loaded, LOADS)
            link(dve.memset(wo_pad[:, :, :, :], 0.0))
            for o in range(CK):
                dve.tensor_tensor(wo_pad[:, o, :, 0:D], w_nat[:, 3, o, :].rearrange("p (h d) -> p h d", d=D),
                                  gateB[:, :].unsqueeze(2).broadcast_to([P, H, D]), ALU.mult)\
                   .then_inc(wo_ready, 1)
            dve.tensor_tensor(w0[:, :, :], kb0[:, 0:CK, :], kb0[:, CK:2 * CK, :], ALU.subtract)
            for dst, src in ((w1, kb1), (w2, kb2)):
                dve.tensor_scalar(dst[:, :, :], src[:, :, :], 2.0, -1.0, ALU.mult, ALU.add)
            dve.tensor_scalar(scales[:, 0:1], scales[:, 0:1], 4.0, None, ALU.mult)
            dve.tensor_scalar(scales[:, 1:2], scales[:, 1:2], 2.0, None, ALU.mult)
            dve.tensor_scalar(bqk[:, 0, :], bqk[:, 0, :], D ** -0.5, None, ALU.mult)
            for n in range(H // 4):
                dve.wait_ge(band_in, 64 * (n + 1))
                if n:
                    dve.wait_ge(band_out, 16 * n)
                parts(lambda s: t_part[:, :, s, :], t_f[:, :, :]).then_inc(band_done, 1)
            dve.wait_ge(ident_done, 3)
            lo = far[:, 0, :].unsqueeze(2).broadcast_to([KB, H, KB])
            hi = far[:, 1, :].unsqueeze(2).broadcast_to([KB, H, KB])
            link(dve.tensor_tensor(f_a[:, :, :], lo, m_lo[:, :].unsqueeze(1).broadcast_to([KB, H, KB]), ALU.mult))
            link(dve.tensor_tensor(f_b[:, :, :], hi, m_hi[:, :].unsqueeze(1).broadcast_to([KB, H, KB]), ALU.mult))
            link(dve.tensor_tensor(f_a[:, :, :], f_a[:, :, :], f_b[:, :, :], ALU.add))
            link(parts(lambda s: f_part[:, s, :, :], f_a[:, :, :]))
            for s in range(3):
                if s:
                    dve.wait_ge(far_out, 16 * (s + 1))
                dve.tensor_copy(f_wide[:, :, :, :],
                                f_part[:, s, :, :].unsqueeze(3).broadcast_to([KB, H, KB, P]))\
                   .then_inc(far_done, 1)

        @block.tensor
        def _(pe):
            pe.wait_ge(loaded, LOADS)
            pe.wait_ge(ident_done, 1)
            for w in range(3):
                for kk in range(CK):
                    for o in range(CK):
                        last = pe.transpose(ps_w[:, w, kk, o * P:(o + 1) * P],
                                            w_nat[:, w, o, kk * P:(kk + 1) * P], ident[:, :])
            last.then_inc(turned, 1)
            pe.wait_ge(wo_ready, CK)
            for q in range(QUADS):
                for o in range(CK):
                    last = pe.transpose(ps_o[:, q, o * P:(o + 1) * P],
                                        wo_pad[:, o, q * HQ:(q + 1) * HQ, :].rearrange("p h d -> p (h d)"),
                                        ident[:, :])
            last.then_inc(turned, 1)

        @block.scalar
        def _(act):
            act.wait_ge(turned, 1)
            for w in range(3):
                act.activation(wT[:, w, :, :], ps_w[:, w, :, :], ACT.Copy)
            act.wait_ge(turned, 2)
            for q in range(QUADS):
                act.activation(woT[:, q, :], ps_o[:, q, :], ACT.Copy)


def project(nc, makers, g):
    sb, psum, sem = makers
    x, ident, wT, w0, w1, w2 = (g[n] for n in ("x", "ident", "wT", "w0", "w1", "w2"))
    bqk, bvB, boB, scales = (g[n] for n in ("bqk", "bvB", "boB", "scales"))
    q_parts, k_parts, v_pad, resid = (g[n] for n in ("q_parts", "k_parts", "v_pad", "resid"))
    C, CK, CT, CH, NCH, F0, F1 = (g[n] for n in ("C", "CK", "CT", "CH", "NCH", "F0", "F1"))
    FK = F0 // P
    QK = 2 * CK
    WIDE = QK + 2 * FK
    SLIM = 2 * CT

    xt = sb("xt", [P, CT, C])
    xbo = sb("xbo", [P, CT, C])
    xn = sb("xn", [P, CT, C])
    stats = sb("stats", [P, CT, 6])
    mv = sb("mv", [P, CT, 2])
    var = sb("var", [P, CT])
    std = sb("std", [P, CT])
    rstd = sb("rstd", [P, CT])
    newt = sb("newt", [P, CT])
    xnT = sb("xnT", [P, CK, CH])
    piece = sb("piece", [P, 2, CH])
    part = sb("part", [P, 2, 3, CH], BF16)
    vt = sb("vt", [P, H, CT, PD])
    h0 = sb("h0", [P, FK, CH])
    h1 = sb("h1", [P, FK, CH])
    res = sb("res", [P, CT, C])
    ps_x = psum("ps_x", [P, CK, CH])
    ps_wide = psum("ps_wide", [P, 2, CH])
    ps_slim = psum("ps_slim", [P, 2, 512])

    x_in = sem("x_in")
    x_used = sem("x_used")
    var_ready = sem("var_ready")
    std_ready = sem("std_ready")
    xn_ready = sem("xn_ready")
    dve_step = sem("dve_step2")
    pool_step = sem("pool_step2")
    xbo_ready = sem("xbo_ready")
    x_turned = sem("x_turned")
    xnT_ready = sem("xnT_ready")
    wide_ready = sem("wide_ready")
    wide_taken = sem("wide_taken")
    slim_ready = sem("slim_ready")
    slim_taken = sem("slim_taken")
    parts_ready = sem("parts_ready")
    parts_out = [sem("parts_out0"), sem("parts_out1")]
    v_out = sem("v_out")
    res_out = sem("res_out")
    hold = holder(sem("tick"))
    DVE_STEPS = CT + CT + 5 + 1

    def chunks(eng, body):
        body(0, True, False)
        with eng.Fori(1, NCH - 1) as c:
            body(c, False, False)
        body(NCH - 1, False, True)

    with nc.Block() as block:

        @block.sync
        def _(sp):
            def load_x(c):
                sp.dma_start(xt[:, :, :], x[c // 2].rearrange("(h t p) e -> h p t e", p=P, h=2)[c % 2])\
                  .then_inc(x_in, 16)

            def body(c, first, last):
                if not last:
                    sp.wait_ge(x_used, 2 * (c + 1))
                    load_x(c + 1)
                for n in range(QK):
                    sp.wait_ge(parts_ready, c * QK + n + 1)
                    dst = (q_parts if n < CK else k_parts)[c // 2].rearrange(
                        "s (m p) (h t) -> h m p s t", p=P, h=2)[c % 2, n % CK]
                    sp.dma_start(dst, part[:, n % 2, :, :]).then_inc(parts_out[n % 2], 16)
                sp.wait_ge(slim_taken, c * SLIM + CT)
                sp.dma_start(v_pad[c // 2].rearrange("p h (f k) d -> f p h (k d)", f=2)[c % 2],
                             vt[:, :, :, :].rearrange("p h k d -> p h (k d)")).then_inc(v_out, 16)
                sp.wait_ge(slim_taken, (c + 1) * SLIM)
                sp.dma_start(resid[c // 2].rearrange("(h t p) e -> h p t e", p=P, h=2)[c % 2], res[:, :, :])\
                  .then_inc(res_out, 16)

            load_x(0)
            chunks(sp, body)
            for n in range(2):
                sp.wait_ge(parts_out[n], 16 * NCH * QK // 2)
            sp.wait_ge(v_out, 16 * NCH)
            sp.wait_ge(res_out, 16 * NCH)

        @block.gpsimd
        def _(pool):
            pool.memset(vt[:, :, :, :], 0.0).then_inc(xbo_ready, 1)

            def add_bias(c):
                hold(pool, x_in, 16 * (c + 1))
                pool.tensor_tensor(xbo[:, :, :], xt[:, :, :],
                                   boB[:, :].unsqueeze(1).broadcast_to([P, CT, C]), ALU.add)\
                    .then_inc(xbo_ready, 1)
                hold(pool, xbo_ready, c + 2)
                pool.sem_inc(x_used, 1)

            def body(c, first, last):
                for n in range(QK):
                    hold(pool, wide_taken, c * WIDE + n + 1)
                    if not (first and n < 2):
                        hold(pool, parts_out[n % 2], 16 * (c * (QK // 2) + n // 2))
                    src, dst = piece[:, n % 2, :], part[:, n % 2, :, :]
                    steps = (c * QK + n) * 4
                    pool.tensor_copy(dst[:, 0, :], src).then_inc(pool_step, 1)
                    hold(pool, pool_step, steps + 1)
                    pool.tensor_tensor(src, src, dst[:, 0, :], ALU.subtract).then_inc(pool_step, 1)
                    hold(pool, pool_step, steps + 2)
                    pool.tensor_copy(dst[:, 1, :], src).then_inc(pool_step, 1)
                    hold(pool, pool_step, steps + 3)
                    pool.tensor_tensor(src, src, dst[:, 1, :], ALU.subtract).then_inc(pool_step, 1)
                    hold(pool, pool_step, steps + 4)
                    pool.tensor_copy(dst[:, 2, :], src).then_inc(parts_ready, 1)
                if not last:
                    hold(pool, slim_taken, (c + 1) * SLIM)
                    add_bias(c + 1)

            add_bias(0)
            chunks(pool, body)

        @block.vector
        def _(dve):
            def norm(c):
                base = c * DVE_STEPS
                hold(dve, x_in, 16 * (c + 1))
                for t in range(CT):
                    dve.bn_stats(stats[:, t, :], xt[:, t, :]).then_inc(dve_step, 1)
                hold(dve, dve_step, base + CT)
                for t in range(CT):
                    dve.bn_aggr(mv[:, t, :], stats[:, t, :]).then_inc(dve_step, 1)
                hold(dve, dve_step, base + 2 * CT)
                dve.tensor_scalar(var[:, :], mv[:, :, 1], EPS, None, ALU.add).then_inc(var_ready, 1)
                hold(dve, std_ready, c + 1)
                dve.reciprocal(rstd[:, :], std[:, :]).then_inc(dve_step, 1)
                hold(dve, dve_step, base + 2 * CT + 1)
                dve.tensor_tensor(newt[:, :], rstd[:, :], rstd[:, :], ALU.mult).then_inc(dve_step, 1)
                hold(dve, dve_step, base + 2 * CT + 2)
                dve.tensor_tensor(newt[:, :], newt[:, :], var[:, :], ALU.mult).then_inc(dve_step, 1)
                hold(dve, dve_step, base + 2 * CT + 3)
                dve.tensor_scalar(newt[:, :], newt[:, :], -0.5, 1.5, ALU.mult, ALU.add).then_inc(dve_step, 1)
                hold(dve, dve_step, base + 2 * CT + 4)
                dve.tensor_tensor(rstd[:, :], rstd[:, :], newt[:, :], ALU.mult).then_inc(dve_step, 1)
                hold(dve, dve_step, base + 2 * CT + 5)
                for t in range(CT):
                    last = dve.tensor_scalar(xn[:, t, :], xt[:, t, :], mv[:, t, 0:1], rstd[:, t:t + 1],
                                             ALU.subtract, ALU.mult)
                    if t == CT - 1:
                        last.then_inc(xn_ready, 1)
                hold(dve, xn_ready, c + 1)
                dve.sem_inc(x_used, 1)
                dve.sem_inc(dve_step, 1)

            def body(c, first, last):
                if not first:
                    hold(dve, v_out, 16 * c)
                for t in range(CT):
                    hold(dve, slim_ready, c * SLIM + t + 1)
                    dve.tensor_tensor(vt[:, :, t, 0:D],
                                      ps_slim[:, t % 2, 0:C].rearrange("p (h d) -> p h d", d=D),
                                      bvB[:, :].rearrange("p (h d) -> p h d", d=D), ALU.add)\
                       .then_inc(slim_taken, 1)
                if not last:
                    hold(dve, x_turned, c + 1)
                    norm(c + 1)
                hold(dve, xbo_ready, c + 2)
                if not first:
                    hold(dve, res_out, 16 * c)
                for t in range(CT):
                    hold(dve, slim_ready, c * SLIM + CT + t + 1)
                    dve.scalar_tensor_tensor(out=res[:, t, :], in0=ps_slim[:, t % 2, 0:C],
                                             scalar=scales[:, 2:3], in1=xbo[:, t, :],
                                             op0=ALU.mult, op1=ALU.add).then_inc(slim_taken, 1)

            norm(0)
            hold(dve, xbo_ready, 1)
            chunks(dve, body)

        @block.scalar
        def _(act):
            def root(c):
                act.wait_ge(var_ready, c + 1)
                act.activation(std[:, :], var[:, :], ACT.Sqrt).then_inc(std_ready, 1)

            def body(c, first, last):
                act.wait_ge(x_turned, c + 1)
                for kk in range(CK):
                    act.activation(xnT[:, kk, :], ps_x[:, kk, :], ACT.Copy).then_inc(xnT_ready, 1)
                for u in range(WIDE):
                    act.wait_ge(wide_ready, c * WIDE + u + 1)
                    src = ps_wide[:, u % 2, :]
                    if u < QK:
                        if not (first and u < 2):
                            act.wait_ge(parts_ready, c * QK + u - 1)
                        w, m = u // CK, u % CK
                        act.activation(piece[:, u % 2, :], src, ACT.Identity, bias=bqk[:, w, m:m + 1],
                                       scale=D ** -0.5 if w == 0 else 1.0).then_inc(wide_taken, 1)
                    else:
                        layer, m = (u - QK) // FK, (u - QK) % FK
                        dst = (h0, h1)[layer]
                        act.activation(dst[:, m, :], src, ACT.Relu, scale=scales[:, layer:layer + 1])\
                           .then_inc(wide_taken, 1)
                    if u == QK and not last:
                        root(c + 1)

            root(0)
            chunks(act, body)

        @block.tensor
        def _(pe):
            def body(c, first, last):
                pe.wait_ge(xn_ready, c + 1)
                if not first:
                    pe.wait_ge(xnT_ready, CK * c)
                for kk in range(CK):
                    for t in range(CT):
                        tr = pe.transpose(ps_x[:, kk, t * P:(t + 1) * P], xn[:, t, kk * P:(kk + 1) * P],
                                          ident[:, :])
                tr.then_inc(x_turned, 1)
                pe.wait_ge(xnT_ready, CK * (c + 1))

                def wide(u, k, lhs, rhs):
                    if not (first and u < 2):
                        pe.wait_ge(wide_taken, c * WIDE + u - 1)
                    for n in range(k):
                        mm = pe.matmul(ps_wide[:, u % 2, :], lhs(n), rhs(n), start=(n == 0), stop=(n == k - 1))
                    mm.then_inc(wide_ready, 1)

                def slim(u, k, lhs, rhs):
                    if not (first and u < 2):
                        pe.wait_ge(slim_taken, c * SLIM + u - 1)
                    for n in range(k):
                        mm = pe.matmul(ps_slim[:, u % 2, 0:C], lhs(n), rhs(n), start=(n == 0), stop=(n == k - 1))
                    mm.then_inc(slim_ready, 1)

                for u in range(QK):
                    w, m = u // CK, u % CK
                    wide(u, CK, lambda n: wT[:, w, n, m * P:(m + 1) * P], lambda n: xnT[:, n, :])
                for t in range(CT):
                    slim(t, CK, lambda n: xnT[:, n, t * P:(t + 1) * P], lambda n: wT[:, 2, n, :])
                for m in range(FK):
                    wide(QK + m, CK, lambda n: w0[:, n, m * P:(m + 1) * P], lambda n: xnT[:, n, :])
                pe.wait_ge(wide_taken, c * WIDE + QK + FK)
                for m in range(FK):
                    wide(QK + FK + m, FK, lambda n: w1[:, n, m * P:(m + 1) * P], lambda n: h0[:, n, :])
                pe.wait_ge(wide_taken, (c + 1) * WIDE)
                for t in range(CT):
                    slim(CT + t, FK, lambda n: h1[:, n, t * P:(t + 1) * P], lambda n: w2[:, n, :])

            chunks(pe, body)


def attend(nc, makers, g):
    sb, psum, sem = makers
    ident, flip, woT, out = (g[n] for n in ("ident", "flip", "woT", "out"))
    toep, q_parts, k_parts, v_pad, far_q, block_of_key, resid = (
        g[n] for n in ("toep", "q_parts", "k_parts", "v_pad", "far_q", "block_of_key", "resid"))
    B, T, C, KB, QUADS, TILES, BW = (g[n] for n in ("B", "T", "C", "KB", "QUADS", "TILES", "BW"))
    NQ = B * QUADS
    NT = NQ * TILES
    K_ROWS = QROWS + 3 * KB
    PV_LAG, OUT_LAG = 9, 11

    q_sb = sb("q_sb", [P, 2, HQ, T], BF16)
    k_sb = sb("k_sb", [P, 2, HQ, T], BF16)
    band = sb("band", [P, 2, HQ, 3, BW], BF16)
    v_sb = sb("v_sb", [P, HQ, KB, PD])
    s_sb = sb("s_sb", [P, 4, T])
    work = sb("work", [P, T])
    e_sb = sb("e_sb", [P, 4, T])
    pT = sb("pT", [P, 2, HQ, KB, P])
    top = sb("top", [P, 4, TOPK])
    neg_max = sb("neg_max", [P, 4])
    den = sb("den", [P, 2, HQ])
    rden = sb("rden", [P, 2, HQ])
    rwide = sb("rwide", [P, HQ, PD])
    oT = sb("oT", [P, P])
    rT = sb("rT", [P, P])
    attnT = sb("attnT", [P, 2, P])
    y = sb("y", [P, 2, C])
    acc = sb("acc", [P, 2, KB, C])
    ps_s = psum("ps_s", [P, 2, T])
    ps_t = psum("ps_t", [P, 2, 512])
    ps_o = psum("ps_o2", [P, 512])
    ps_y = psum("ps_y", [P, 512])

    qkt_in = [sem("qkt_in0"), sem("qkt_in1")]
    v_in = sem("v_in")
    once_in = sem("once_in")
    acc_in = sem("acc_in")
    out_sent = sem("out_sent")
    s_ready = sem("s_ready")
    s_taken = sem("s_taken")
    top_step = sem("top_step")
    max_ready = sem("max_ready")
    neg_ready = sem("neg_ready")
    e_ready = sem("e_ready")
    p_ready = sem("p_ready")
    p_turned = sem("p_turned")
    pT_ready = sem("pT_ready")
    rden_ready = sem("rden_ready")
    rwide_ready = sem("rwide_ready")
    pv_ready = sem("pv_ready")
    pv_taken = sem("pv_taken")
    attn_ready = sem("attn_ready")
    y_ready = sem("y_ready")
    y_taken = sem("y_taken")
    acc_ready = sem("acc_ready")
    hold = holder(sem("tick2"))
    QKT = 16 * (2 * len(PAIRS) + 2)

    def quads(eng, body, lag):
        for i in range(TILES):
            body(0, i, True)
        with eng.Fori(1, NQ) as q:
            for i in range(TILES):
                body(q, i, False)
        if lag:
            for i in range(lag):
                body(NQ, i, False)

    with nc.Block() as block:

        @block.sync
        def _(sp):
            def load_qkt(b, hq, slot):
                h = HQ * hq
                sem_ = qkt_in[slot]
                for r, (a, c) in enumerate(PAIRS):
                    for dst, src, s in ((q_sb, q_parts, a), (k_sb, k_parts, c)):
                        sp.dma_start(dst[D * r:D * (r + 1), slot, :, :],
                                     src[b, s, h * D:(h + HQ) * D, :].rearrange("(j d) t -> d j t", d=D))\
                          .then_inc(sem_, 16)
                sp.dma_start(q_sb[QROWS:K_ROWS, slot, :, :],
                             far_q[:, :, h:h + HQ, :].rearrange("s r j t -> (s r) j t")).then_inc(sem_, 16)
                sp.dma_start(band[:, slot, :, :, :].rearrange("p j s c -> p j (s c)"),
                             toep[h:h + HQ].rearrange("h p c -> p h c")).then_inc(sem_, 16)

            def load_v(b, hq):
                sp.dma_start(v_sb[:, :, :, :].rearrange("p j k d -> p (j k d)"),
                             v_pad[b, :, HQ * hq:HQ * (hq + 1)].rearrange("p j k d -> p (j k d)"))\
                  .then_inc(v_in, 16)

            def load_acc(b, slot):
                sp.dma_start(acc[:, slot, :, :], resid[b].rearrange("(t p) e -> p t e", p=P)).then_inc(acc_in, 16)

            def send(b, slot):
                sp.wait_ge(acc_ready, (b + 1) * QUADS * KB)
                sp.dma_start(out[b].rearrange("(t p) e -> p t e", p=P), acc[:, slot, :, :]).then_inc(out_sent, 16)
                sp.wait_ge(out_sent, 16 * (b + 1))

            for s in range(3):
                sp.dma_start(k_sb[QROWS + KB * s:QROWS + KB * (s + 1), :, :, :].rearrange("r a j t -> r (a j) t"),
                             block_of_key.unsqueeze(1).broadcast_to([KB, 2 * HQ, T])).then_inc(once_in, 16)
            load_qkt(0, 0, 0)
            load_v(0, 0)
            load_acc(0, 0)
            load_qkt(0, 1, 1)

            def batch(b, first, last):
                for hq in range(QUADS):
                    n = b * QUADS + hq
                    if not (first and hq == 0):
                        sp.wait_ge(pv_ready, n * KB)
                        load_v(b, hq)
                        if not (last and hq == QUADS - 1):
                            sp.wait_ge(s_ready, n * TILES)
                            nh = (hq + 1) % QUADS
                            load_qkt(b + (1 if nh == 0 else 0), nh, nh % 2)
                    if hq == 1:
                        if not first:
                            send(b - 1, (b + 1) % 2)
                        if not last:
                            load_acc(b + 1, (b + 1) % 2)

            batch(0, True, False)
            with sp.Fori(1, B - 1) as b:
                batch(b, False, False)
            batch(B - 1, False, True)
            send(B - 1, (B - 1) % 2)

        @block.tensor
        def _(pe):
            def scores(q, i):
                qi, j, slot = i // HQ, i % HQ, q % 2
                t = q * TILES + i
                ps = ps_s[:, i % 2, :]
                near = range(max(qi - 3, 0), min(qi + 2, KB))
                for half in range(2):
                    blocks = [k for k in near if k // 4 == half]
                    mm = pe.matmul(ps[:, half * 512:(half + 1) * 512],
                                   q_sb[0:K_ROWS, slot, j, qi * P:(qi + 1) * P],
                                   k_sb[0:K_ROWS, slot, j, half * 512:(half + 1) * 512],
                                   start=True, stop=not blocks)
                    for s in range(3 if blocks else 0):
                        c = (blocks[0] - qi + 3) * P
                        w = len(blocks) * P
                        mm = pe.matmul(ps[:, blocks[0] * P:blocks[0] * P + w], flip[:, :],
                                       band[:, slot, j, s, c:c + w], start=False, stop=(s == 2))
                mm.then_inc(s_ready, 1)

            def turn(t, i):
                for half in range(2):
                    if not (isinstance(t, int) and t == 0):
                        pe.wait_ge(pT_ready, 2 * t - 1 + half)
                    for k in range(4 * half, 4 * half + 4):
                        tr = pe.transpose(ps_t[:, half, (k % 4) * P:(k % 4 + 1) * P],
                                          e_sb[:, i % 4, k * P:(k + 1) * P], ident[:, :])
                    tr.then_inc(p_turned, 1)

            def body(q, i, first):
                t = q * TILES + i
                over = isinstance(q, int) and q == NQ
                if not over:
                    if i == 0:
                        if first:
                            pe.wait_ge(once_in, 48)
                        if isinstance(q, int):
                            pe.wait_ge(qkt_in[q % 2], QKT * (q // 2 + 1))
                        else:
                            pe.wait_ge(qkt_in[0], QKT * ((q + 2) // 2))
                            pe.wait_ge(qkt_in[1], QKT * ((q + 1) // 2))
                    if not (first and i < 2):
                        pe.wait_ge(s_taken, t - 1)
                    scores(q, i)
                if not (first and i < 4) and not (over and i >= 4):
                    pe.wait_ge(p_ready, t - 3)
                    turn(t - 4, i)
                if i % HQ == PV_LAG % HQ and not (first and i < PV_LAG) and not (over and i >= PV_LAG):
                    m = q * KB + (i - PV_LAG) // HQ
                    mp = ((i - PV_LAG) // HQ) % 2
                    if i == PV_LAG:
                        pe.wait_ge(v_in, 16 * (q + 1))
                    pe.wait_ge(pT_ready, 2 * HQ * (m + 1))
                    if not (first and i == PV_LAG):
                        pe.wait_ge(pv_taken, m)
                    for k in range(KB):
                        for j in range(HQ):
                            mm = pe.matmul(ps_o[PD * j:PD * (j + 1), 0:P], v_sb[:, j, k, :], pT[:, mp, j, k, :],
                                           start=(k == 0), stop=(k == KB - 1))
                    pe.wait_ge(rwide_ready, m + 1)
                    mm = pe.transpose(ps_o[:, P:2 * P], rwide[:, :, :].rearrange("p j d -> p (j d)"), ident[:, :])
                    mm.then_inc(pv_ready, 1)
                if i % HQ == OUT_LAG % HQ and not (first and i < OUT_LAG) and not (over and i >= OUT_LAG):
                    m = q * KB + (i - OUT_LAG) // HQ
                    mp = ((i - OUT_LAG) // HQ) % 2
                    hq = q % QUADS if i >= OUT_LAG else (q + QUADS - 1) % QUADS
                    pe.wait_ge(attn_ready, m + 1)
                    if not (first and i == OUT_LAG):
                        pe.wait_ge(y_taken, m)
                    pe.matmul(ps_y[:, 0:C], attnT[:, mp, :], woT[:, hq, :], start=True, stop=True)\
                      .then_inc(y_ready, 1)

            quads(pe, body, OUT_LAG)

        @block.scalar
        def _(act):
            def body(q, i, first):
                t = q * TILES + i
                over = isinstance(q, int) and q == NQ
                if not over:
                    act.wait_ge(s_ready, t + 1)
                    if not (first and i < 4):
                        act.wait_ge(p_ready, t - 3)
                    act.activation(s_sb[:, i % 4, :], ps_s[:, i % 2, :], ACT.Copy).then_inc(s_taken, 1)
                if not (first and i < 2) and not (over and i >= 2):
                    act.wait_ge(neg_ready, t - 1)
                    if not (first and i < 6):
                        act.wait_ge(p_turned, 2 * (t - 5))
                    act.activation(e_sb[:, (i - 2) % 4, :], s_sb[:, (i - 2) % 4, :], ACT.Exp,
                                   bias=neg_max[:, (i - 2) % 4:(i - 2) % 4 + 1]).then_inc(e_ready, 1)
                if not (first and i < 4) and not (over and i >= 4):
                    mp, j = ((i - 4) // HQ) % 2, i % HQ
                    if not (first and i < 12):
                        act.wait_ge(pv_ready, q * KB + (i - 12) // HQ + 1)
                    for half in range(2):
                        act.wait_ge(p_turned, 2 * (t - 4) + 1 + half)
                        act.activation(pT[:, mp, j, 4 * half:4 * half + 4, :], ps_t[:, half, :], ACT.Copy)\
                           .then_inc(pT_ready, 1)
                if i % HQ == (PV_LAG + 1) % HQ and not (first and i < PV_LAG + 1) and not (over and i > PV_LAG):
                    m = q * KB + (i - PV_LAG - 1) // HQ
                    act.wait_ge(pv_ready, m + 1)
                    if not (first and i == PV_LAG + 1):
                        act.wait_ge(attn_ready, m)
                    act.activation(oT[:, :], ps_o[:, 0:P], ACT.Copy)
                    act.activation(rT[:, :], ps_o[:, P:2 * P], ACT.Copy).then_inc(pv_taken, 1)
                if i % HQ == OUT_LAG % HQ and not (first and i < OUT_LAG + HQ):
                    m = q * KB + (i - OUT_LAG - HQ) // HQ
                    act.wait_ge(y_ready, m + 1)
                    if not (first and i < OUT_LAG + 3 * HQ):
                        act.wait_ge(acc_ready, m - 1)
                    act.activation(y[:, ((i - OUT_LAG - HQ) // HQ) % 2, :], ps_y[:, 0:C], ACT.Copy)\
                       .then_inc(y_taken, 1)

            quads(act, body, OUT_LAG + HQ)

        @block.gpsimd
        def _(pool):
            def body(q, i, first):
                t = q * TILES + i
                over = isinstance(q, int) and q == NQ
                if not over:
                    hold(pool, max_ready, t + 1)
                    if not (first and i < 4):
                        hold(pool, e_ready, t - 3)
                    pool.tensor_scalar(neg_max[:, i % 4:i % 4 + 1], top[:, i % 4, 0:1], -1.0, None, ALU.mult)\
                        .then_inc(neg_ready, 1)
                if i % HQ == 0 and not (first and i < HQ):
                    m = q * KB + i // HQ - 1
                    if not (over and i > 0):
                        hold(pool, rden_ready, m + 1)
                        if not (first and i < 2 * HQ):
                            hold(pool, pv_ready, m)
                        pool.tensor_copy(rwide[:, :, :],
                                         rden[:, (i // HQ - 1) % 2, :].unsqueeze(2).broadcast_to([P, HQ, PD]))\
                            .then_inc(rwide_ready, 1)
                if i % HQ == (PV_LAG + 1) % HQ and not (first and i < PV_LAG + 1) and not (over and i > PV_LAG):
                    m = q * KB + (i - PV_LAG - 1) // HQ
                    mp = ((i - PV_LAG - 1) // HQ) % 2
                    hold(pool, pv_taken, m + 1)
                    if not (first and i < PV_LAG + 1 + 2 * HQ):
                        hold(pool, y_ready, m - 1)
                    pool.tensor_tensor(attnT[:, mp, :], oT[:, :], rT[:, :], ALU.mult).then_inc(attn_ready, 1)
                if i % HQ == (OUT_LAG + 1) % HQ and not (first and i < OUT_LAG + 1 + HQ):
                    m = q * KB + (i - OUT_LAG - HQ - 1) // HQ
                    tile = (i - OUT_LAG - HQ - 1) // HQ
                    batch = (q // QUADS) if tile >= 0 else ((q + QUADS - 1) // QUADS - 1)
                    batch = (m // (KB * QUADS))
                    if tile % KB == 0:
                        hold(pool, acc_in, 16 * (batch + 1))
                    hold(pool, y_taken, m + 1)
                    a = acc[:, batch % 2, tile % KB, :]
                    pool.tensor_tensor(a, a, y[:, tile % 2, :], ALU.add).then_inc(acc_ready, 1)

            quads(pool, body, OUT_LAG + HQ)

        @block.vector
        def _(dve):
            STEPS = 6

            def body(q, i, first):
                t = q * TILES + i
                over = isinstance(q, int) and q == NQ
                s, w, tp = s_sb[:, i % 4, :], work[:, :], top[:, i % 4, :]
                hold(dve, s_taken, t + 1)
                if not (first and i < 4):
                    hold(dve, neg_ready, t - 3)
                dve.max(tp[:, 0:8], s).then_inc(max_ready, 1)
                hold(dve, max_ready, t + 1)
                for n in range(1, TOPK // 8):
                    dve.match_replace(w, tp[:, 8 * n - 8:8 * n], s if n == 1 else w, NEG).then_inc(top_step, 1)
                    dve.wait_ge(top_step, 2 * n - 1)
                    dve.max(tp[:, 8 * n:8 * n + 8], w).then_inc(top_step, 1)
                    dve.wait_ge(top_step, 2 * n)
                dve.wait_ge(e_ready, t + 1)
                dve.sem_inc(top_step, -STEPS)
                e = e_sb[:, i % 4, :]
                mp, j = (i // HQ) % 2, i % HQ
                dve.scalar_tensor_tensor(out=e, in0=s, scalar=tp[:, TOPK - 1:TOPK], in1=e, op0=ALU.is_ge,
                                         op1=ALU.mult, accum_out=den[:, mp, j:j + 1]).then_inc(p_ready, 1)
                if j == HQ - 1:
                    hold(dve, p_ready, t + 1)
                    if not (first and i < 3 * HQ):
                        hold(dve, rwide_ready, q * KB + i // HQ - 1)
                    dve.reciprocal(rden[:, mp, :], den[:, mp, :]).then_inc(rden_ready, 1)

            quads(dve, body, 0)


_INS = ["L0_attn_x", "L0_attn_Wq", "L0_attn_bq", "L0_attn_Wk", "L0_attn_bk", "L0_attn_Wv", "L0_attn_bv",
        "L0_attn_Wo", "L0_attn_bo", "L0_attn_head_gates", "L0_attn_rel_bias", "L0_ffn_k0", "L0_ffn_k1",
        "L0_ffn_k2", "L0_ffn_s0", "L0_ffn_s1", "L0_ffn_s2"]


def kernel(**inputs):
    import numpy as _np
    import concourse.bacc as _bacc
    from concourse import mybir as _mybir
    from concourse.bass_utils import run_bass_kernel_spmd as _run

    nc = _bacc.Bacc("TRN2", target_bir_lowering=False, num_devices=1)
    arrays, args = {}, []
    for name in _INS:
        a = _np.ascontiguousarray(inputs[name])
        a = a.reshape(a.shape or (1,))
        arrays[f"in_{name}_dram"] = a
        args.append(nc.dram_tensor(f"in_{name}_dram", a.shape, _mybir.dt.from_np(a.dtype), kind="ExternalInput").ap())
    out = nc.dram_tensor("out_0_dram", inputs["L0_attn_x"].shape, F32, kind="ExternalOutput").ap()
    attention_ffn_kernel(nc, *args, out)
    r = _run(nc, [arrays], core_ids=[0])
    return r.results[0]["out_0_dram"]
```

```python
from contextlib import ExitStack

import concourse.bass as bass
from concourse import mybir

F32 = mybir.dt.float32
BF16 = mybir.dt.bfloat16
U8 = mybir.dt.uint8
ALU = mybir.AluOpType
ACT = mybir.ActivationFunctionType

P = 128
H, D = 16, 16
TOPK = 32
MAXPOS = 128
EPS = 1e-5
NEG = -3.0e38
CHUNKS = 24
HQ = 4
PD = 32
BAND = 5
QROWS = 96
PAIRS = [(0, 0), (0, 1), (1, 0), (1, 1), (0, 2), (2, 0)]


def holder(tick):
    def hold(eng, sem, value):
        eng.wait_ge(sem, value)
        if not isinstance(value, int):
            eng.sem_inc(tick, 1)
    return hold


def attention_ffn_kernel(nc, x, Wq, bq, Wk, bk, Wv, bv, Wo, bo, gates, rel, k0, k1, k2, s0, s1, s2, out):
    B, T, C = x.shape
    F0, F1 = k0.shape[1], k1.shape[1]
    KB = T // P
    NCH = B * 2
    CH = T // 2
    CT = CH // P
    CK = C // P
    QUADS = H // HQ
    TILES = KB * HQ
    BW = BAND * P
    FV = T // 2 + 2 * P
    assert CK == 2 and H * D == C and F0 == 1024 and F1 == 1024

    fvec = nc.dram_tensor("fvec", [H, FV], F32).ap()
    toep = nc.dram_tensor("toep", [H, P, 3 * BW], BF16).ap()
    q_parts = nc.dram_tensor("q_parts", [B, 3, C, T], BF16).ap()
    k_parts = nc.dram_tensor("k_parts", [B, 3, C, T], BF16).ap()
    v_pad = nc.dram_tensor("v_pad", [B, P, H, KB, PD], F32).ap()
    far_q = nc.dram_tensor("far_q", [3, KB, H, T], BF16).ap()
    block_of_key = nc.dram_tensor("block_of_key", [KB, T], BF16).ap()
    resid = nc.dram_tensor("resid", [B, T, C], F32).ap()

    nc.disable_value_cache = True
    with ExitStack() as whole:
        def tensors(ctx):
            return (lambda n, s, d=F32: ctx.enter_context(nc.sbuf_tensor(n, s, d)),
                    lambda n, s, d=F32: ctx.enter_context(nc.psum_tensor(n, s, d)),
                    lambda n: ctx.enter_context(nc.semaphore(n)))

        sb, _, _ = tensors(whole)
        ident = sb("ident", [P, P])
        flip = sb("flip", [P, P], BF16)
        woT = sb("woT", [P, QUADS, C])
        with ExitStack() as early:
            sbe, _, _ = tensors(early)
            wT = sbe("wT", [P, 3, CK, C])
            w0 = sbe("w0", [P, CK, F0])
            w1 = sbe("w1", [P, F0 // P, F1])
            w2 = sbe("w2", [P, F1 // P, C])
            bqk = sbe("bqk", [P, 2, CK])
            bvB = sbe("bvB", [P, C])
            boB = sbe("boB", [P, C])
            scales = sbe("scales", [P, 3])
            with ExitStack() as ctx:
                setup(nc, tensors(ctx), locals())
            with ExitStack() as ctx:
                project(nc, tensors(ctx), locals())
        with ExitStack() as ctx:
            attend(nc, tensors(ctx), locals())


def setup(nc, makers, g):
    sb, psum, sem = makers
    x, Wq, bq, Wk, bk, Wv, bv, Wo, bo = (g[n] for n in ("x", "Wq", "bq", "Wk", "bk", "Wv", "bv", "Wo", "bo"))
    gates, rel, k0, k1, k2, s0, s1, s2 = (g[n] for n in ("gates", "rel", "k0", "k1", "k2", "s0", "s1", "s2"))
    ident, flip, woT, wT, w0, w1, w2 = (g[n] for n in ("ident", "flip", "woT", "wT", "w0", "w1", "w2"))
    bqk, bvB, boB, scales = (g[n] for n in ("bqk", "bvB", "boB", "scales"))
    fvec, toep, far_q, block_of_key = (g[n] for n in ("fvec", "toep", "far_q", "block_of_key"))
    C, T, KB, CK, QUADS, BW, FV = (g[n] for n in ("C", "T", "KB", "CK", "QUADS", "BW", "FV"))
    NR = 2 * MAXPOS - 1

    w_nat = sb("w_nat", [P, 4, CK, C])
    kb0 = sb("kb0", [P, 2 * CK, 1024], U8)
    kb1 = sb("kb1", [P, 8, 1024], U8)
    kb2 = sb("kb2", [P, 8, C], U8)
    gateB = sb("gateB", [P, H])
    wo_pad = sb("wo_pad", [P, CK, H, PD])
    relT = sb("relT", [H, NR])
    fv = sb("fv", [H, FV])
    far = sb("far", [KB, 2, H])
    m_lo = sb("m_lo", [KB, KB])
    m_hi = sb("m_hi", [KB, KB])
    f_a = sb("f_a", [KB, H, KB])
    f_b = sb("f_b", [KB, H, KB])
    f_part = sb("f_part", [KB, 3, H, KB], BF16)
    f_wide = sb("f_wide", [KB, H, KB, P], BF16)
    onehot = sb("onehot", [KB, KB, P], BF16)
    t_f = sb("t_f", [P, 4, BW])
    t_part = sb("t_part", [P, 4, 3, BW], BF16)
    ps_w = psum("ps_w", [P, 3, CK, C])
    ps_o = psum("ps_o", [P, QUADS, C])

    loaded = sem("loaded")
    rel_loaded = sem("rel_loaded")
    table_done = sem("table_done")
    table_out = sem("table_out")
    band_in = sem("band_in")
    band_done = sem("band_done")
    band_out = sem("band_out")
    far_done = sem("far_done")
    far_out = sem("far_out")
    ident_done = sem("ident_done")
    pool_step = sem("pool_step")
    dve_step = sem("dve_step")
    wo_ready = sem("wo_ready")
    turned = sem("turned")
    LOADS = 15 * 16

    with nc.Block() as block:

        @block.sync
        def _(sp):
            with nc.allow_non_contiguous_dma("short vectors"):
                sp.dma_start(relT[:, :], rel.rearrange("r h -> h r")).then_inc(rel_loaded, 16)
                sp.dma_start(far[:, 0, :], rel[0, :].partition_broadcast(KB)).then_inc(rel_loaded, 16)
                sp.dma_start(far[:, 1, :], rel[NR - 1, :].partition_broadcast(KB)).then_inc(rel_loaded, 16)
                for n, w in enumerate((Wq, Wk, Wv, Wo)):
                    sp.dma_start(w_nat[:, n, :, :], w.rearrange("(o p) i -> p o i", p=P)).then_inc(loaded, 16)
                for dst, src in ((kb0, k0), (kb1, k1), (kb2, k2)):
                    sp.dma_start(dst[:, :, :], src.rearrange("(k p) n -> p k n", p=P)).then_inc(loaded, 16)
                for n, b in enumerate((bq, bk)):
                    sp.dma_start(bqk[:, n, :], b.rearrange("(m p) -> p m", p=P)).then_inc(loaded, 16)
                sp.dma_start(bvB[:, :], bv.partition_broadcast(P)).then_inc(loaded, 16)
                sp.dma_start(boB[:, :], bo.partition_broadcast(P)).then_inc(loaded, 16)
                sp.dma_start(gateB[:, :], gates.partition_broadcast(P)).then_inc(loaded, 16)
                for n, s in enumerate((s0, s1, s2)):
                    sp.dma_start(scales[:, n:n + 1], s.partition_broadcast(P)).then_inc(loaded, 16)
            sp.wait_ge(table_done, 1)
            sp.dma_start(fvec, fv[:, :]).then_inc(table_out, 16)
            sp.wait_ge(table_out, 16)
            for n in range(H // 4):
                if n:
                    sp.wait_ge(band_done, n)
                for h in range(4 * n, 4 * n + 4):
                    src = bass.AP(tensor=fvec.tensor, offset=h * FV, ap=[[1, P], [1, BW]])
                    sp.dma_start(t_f[:, h % 4, :], src).then_inc(band_in, 16)
                sp.wait_ge(band_done, n + 1)
                sp.dma_start(toep[4 * n:4 * n + 4].rearrange("h p c -> p h c"),
                             t_part[:, :, :, :].rearrange("p h s c -> p h (s c)")).then_inc(band_out, 16)
            sp.wait_ge(ident_done, 3)
            sp.dma_start(block_of_key, onehot[:, :, :].rearrange("r b c -> r (b c)")).then_inc(far_out, 16)
            for s in range(3):
                sp.wait_ge(far_done, s + 1)
                sp.dma_start(far_q[s], f_wide[:, :, :, :].rearrange("r h i c -> r h (i c)")).then_inc(far_out, 16)
            sp.wait_ge(far_out, 64)
            sp.wait_ge(band_out, 16 * (H // 4))

        @block.gpsimd
        def _(pool):
            def link(ins, count=[0]):
                count[0] += 1
                ins.then_inc(pool_step, 1)
                pool.wait_ge(pool_step, count[0])

            link(pool.memset(ident[:, :], 0.0))
            pool.affine_select(out=ident[:, :], in_=ident[:, :], compare_op=ALU.not_equal, fill=1.0,
                               base=0, pattern=[[-1, P]], channel_multiplier=1).then_inc(ident_done, 1)
            link(pool.memset(flip[:, :], 0.0))
            pool.affine_select(out=flip[:, :], in_=flip[:, :], compare_op=ALU.not_equal, fill=1.0,
                               base=1 - P, pattern=[[1, P]], channel_multiplier=1)
            link(pool.memset(onehot[:, :, :], 1.0))
            pool.affine_select(out=onehot[:, :, :], in_=onehot[:, :, :], compare_op=ALU.is_equal, fill=0.0,
                               base=0, pattern=[[-1, KB], [0, P]], channel_multiplier=1).then_inc(ident_done, 1)
            link(pool.memset(m_lo[:, :], 1.0))
            link(pool.memset(m_hi[:, :], 1.0))
            link(pool.affine_select(out=m_lo[:, :], in_=m_lo[:, :], compare_op=ALU.is_ge, fill=0.0,
                                    base=-4, pattern=[[1, KB]], channel_multiplier=-1))
            pool.affine_select(out=m_hi[:, :], in_=m_hi[:, :], compare_op=ALU.is_ge, fill=0.0,
                               base=-2, pattern=[[-1, KB]], channel_multiplier=1).then_inc(ident_done, 1)

        @block.vector
        def _(dve):
            def link(ins, count=[0]):
                count[0] += 1
                ins.then_inc(dve_step, 1)
                dve.wait_ge(dve_step, count[0])

            def parts(dst, src):
                link(dve.tensor_copy(dst(0), src))
                link(dve.tensor_tensor(src, src, dst(0), ALU.subtract))
                link(dve.tensor_copy(dst(1), src))
                link(dve.tensor_tensor(src, src, dst(1), ALU.subtract))
                return dve.tensor_copy(dst(2), src)

            dve.wait_ge(rel_loaded, 48)
            a = FV - 1 - P - 2 * NR
            dve.tensor_copy(fv[:, 0:a], relT[:, 0:1].broadcast_to([H, a]))
            dve.tensor_copy(fv[:, a:a + NR], relT[:, :])
            dve.tensor_copy(fv[:, a + NR:a + 2 * NR], relT[:, :])
            dve.tensor_copy(fv[:, a + 2 * NR:FV], relT[:, NR - 1:NR].broadcast_to([H, FV - a - 2 * NR]))\
               .then_inc(table_done, 1)
            dve.wait_ge(loaded, LOADS)
            link(dve.memset(wo_pad[:, :, :, :], 0.0))
            for o in range(CK):
                dve.tensor_tensor(wo_pad[:, o, :, 0:D], w_nat[:, 3, o, :].rearrange("p (h d) -> p h d", d=D),
                                  gateB[:, :].unsqueeze(2).broadcast_to([P, H, D]), ALU.mult)\
                   .then_inc(wo_ready, 1)
            dve.tensor_tensor(w0[:, :, :], kb0[:, 0:CK, :], kb0[:, CK:2 * CK, :], ALU.subtract)
            for dst, src in ((w1, kb1), (w2, kb2)):
                dve.tensor_scalar(dst[:, :, :], src[:, :, :], 2.0, -1.0, ALU.mult, ALU.add)
            dve.tensor_scalar(scales[:, 0:1], scales[:, 0:1], 4.0, None, ALU.mult)
            dve.tensor_scalar(scales[:, 1:2], scales[:, 1:2], 2.0, None, ALU.mult)
            dve.tensor_scalar(bqk[:, 0, :], bqk[:, 0, :], D ** -0.5, None, ALU.mult)
            for n in range(H // 4):
                dve.wait_ge(band_in, 64 * (n + 1))
                if n:
                    dve.wait_ge(band_out, 16 * n)
                parts(lambda s: t_part[:, :, s, :], t_f[:, :, :]).then_inc(band_done, 1)
            dve.wait_ge(ident_done, 3)
            lo = far[:, 0, :].unsqueeze(2).broadcast_to([KB, H, KB])
            hi = far[:, 1, :].unsqueeze(2).broadcast_to([KB, H, KB])
            link(dve.tensor_tensor(f_a[:, :, :], lo, m_lo[:, :].unsqueeze(1).broadcast_to([KB, H, KB]), ALU.mult))
            link(dve.tensor_tensor(f_b[:, :, :], hi, m_hi[:, :].unsqueeze(1).broadcast_to([KB, H, KB]), ALU.mult))
            link(dve.tensor_tensor(f_a[:, :, :], f_a[:, :, :], f_b[:, :, :], ALU.add))
            link(parts(lambda s: f_part[:, s, :, :], f_a[:, :, :]))
            for s in range(3):
                if s:
                    dve.wait_ge(far_out, 16 * (s + 1))
                dve.tensor_copy(f_wide[:, :, :, :],
                                f_part[:, s, :, :].unsqueeze(3).broadcast_to([KB, H, KB, P]))\
                   .then_inc(far_done, 1)

        @block.tensor
        def _(pe):
            pe.wait_ge(loaded, LOADS)
            pe.wait_ge(ident_done, 1)
            for w in range(3):
                for kk in range(CK):
                    for o in range(CK):
                        last = pe.transpose(ps_w[:, w, kk, o * P:(o + 1) * P],
                                            w_nat[:, w, o, kk * P:(kk + 1) * P], ident[:, :])
            last.then_inc(turned, 1)
            pe.wait_ge(wo_ready, CK)
            for q in range(QUADS):
                for o in range(CK):
                    last = pe.transpose(ps_o[:, q, o * P:(o + 1) * P],
                                        wo_pad[:, o, q * HQ:(q + 1) * HQ, :].rearrange("p h d -> p (h d)"),
                                        ident[:, :])
            last.then_inc(turned, 1)

        @block.scalar
        def _(act):
            act.wait_ge(turned, 1)
            for w in range(3):
                act.activation(wT[:, w, :, :], ps_w[:, w, :, :], ACT.Copy)
            act.wait_ge(turned, 2)
            for q in range(QUADS):
                act.activation(woT[:, q, :], ps_o[:, q, :], ACT.Copy)


def project(nc, makers, g):
    sb, psum, sem = makers
    x, ident, wT, w0, w1, w2 = (g[n] for n in ("x", "ident", "wT", "w0", "w1", "w2"))
    bqk, bvB, boB, scales = (g[n] for n in ("bqk", "bvB", "boB", "scales"))
    q_parts, k_parts, v_pad, resid = (g[n] for n in ("q_parts", "k_parts", "v_pad", "resid"))
    C, CK, CT, CH, NCH, F0, F1 = (g[n] for n in ("C", "CK", "CT", "CH", "NCH", "F0", "F1"))
    FK = F0 // P
    QK = 2 * CK
    WIDE = QK + 2 * FK
    SLIM = 2 * CT

    xt = sb("xt", [P, CT, C])
    xbo = sb("xbo", [P, CT, C])
    xn = sb("xn", [P, CT, C])
    stats = sb("stats", [P, CT, 6])
    mv = sb("mv", [P, CT, 2])
    var = sb("var", [P, CT])
    std = sb("std", [P, CT])
    rstd = sb("rstd", [P, CT])
    newt = sb("newt", [P, CT])
    xnT = sb("xnT", [P, CK, CH])
    piece = sb("piece", [P, 2, CH])
    part = sb("part", [P, 2, 3, CH], BF16)
    vt = sb("vt", [P, H, CT, PD])
    h0 = sb("h0", [P, FK, CH])
    h1 = sb("h1", [P, FK, CH])
    res = sb("res", [P, CT, C])
    ps_x = psum("ps_x", [P, CK, CH])
    ps_wide = psum("ps_wide", [P, 2, CH])
    ps_slim = psum("ps_slim", [P, 2, 512])

    x_in = sem("x_in")
    x_used = sem("x_used")
    var_ready = sem("var_ready")
    std_ready = sem("std_ready")
    xn_ready = sem("xn_ready")
    dve_step = sem("dve_step2")
    pool_step = sem("pool_step2")
    xbo_ready = sem("xbo_ready")
    x_turned = sem("x_turned")
    xnT_ready = sem("xnT_ready")
    wide_ready = sem("wide_ready")
    wide_taken = sem("wide_taken")
    slim_ready = sem("slim_ready")
    slim_taken = sem("slim_taken")
    parts_ready = sem("parts_ready")
    parts_out = [sem("parts_out0"), sem("parts_out1")]
    v_out = sem("v_out")
    res_out = sem("res_out")
    hold = holder(sem("tick"))
    DVE_STEPS = CT + CT + 5 + 1

    def chunks(eng, body):
        body(0, True, False)
        with eng.Fori(1, NCH - 1) as c:
            body(c, False, False)
        body(NCH - 1, False, True)

    with nc.Block() as block:

        @block.sync
        def _(sp):
            def load_x(c):
                sp.dma_start(xt[:, :, :], x[c // 2].rearrange("(h t p) e -> h p t e", p=P, h=2)[c % 2])\
                  .then_inc(x_in, 16)

            def body(c, first, last):
                if not last:
                    sp.wait_ge(x_used, 2 * (c + 1))
                    load_x(c + 1)
                for n in range(QK):
                    sp.wait_ge(parts_ready, c * QK + n + 1)
                    dst = (q_parts if n < CK else k_parts)[c // 2].rearrange(
                        "s (m p) (h t) -> h m p s t", p=P, h=2)[c % 2, n % CK]
                    sp.dma_start(dst, part[:, n % 2, :, :]).then_inc(parts_out[n % 2], 16)
                sp.wait_ge(slim_taken, c * SLIM + CT)
                sp.dma_start(v_pad[c // 2].rearrange("p h (f k) d -> f p h (k d)", f=2)[c % 2],
                             vt[:, :, :, :].rearrange("p h k d -> p h (k d)")).then_inc(v_out, 16)
                sp.wait_ge(slim_taken, (c + 1) * SLIM)
                sp.dma_start(resid[c // 2].rearrange("(h t p) e -> h p t e", p=P, h=2)[c % 2], res[:, :, :])\
                  .then_inc(res_out, 16)

            load_x(0)
            chunks(sp, body)
            for n in range(2):
                sp.wait_ge(parts_out[n], 16 * NCH * QK // 2)
            sp.wait_ge(v_out, 16 * NCH)
            sp.wait_ge(res_out, 16 * NCH)

        @block.gpsimd
        def _(pool):
            pool.memset(vt[:, :, :, :], 0.0).then_inc(xbo_ready, 1)

            def add_bias(c):
                hold(pool, x_in, 16 * (c + 1))
                pool.tensor_tensor(xbo[:, :, :], xt[:, :, :],
                                   boB[:, :].unsqueeze(1).broadcast_to([P, CT, C]), ALU.add)\
                    .then_inc(xbo_ready, 1)
                hold(pool, xbo_ready, c + 2)
                pool.sem_inc(x_used, 1)

            def body(c, first, last):
                for n in range(QK):
                    hold(pool, wide_taken, c * WIDE + n + 1)
                    if not (first and n < 2):
                        hold(pool, parts_out[n % 2], 16 * (c * (QK // 2) + n // 2))
                    src, dst = piece[:, n % 2, :], part[:, n % 2, :, :]
                    steps = (c * QK + n) * 4
                    pool.tensor_copy(dst[:, 0, :], src).then_inc(pool_step, 1)
                    hold(pool, pool_step, steps + 1)
                    pool.tensor_tensor(src, src, dst[:, 0, :], ALU.subtract).then_inc(pool_step, 1)
                    hold(pool, pool_step, steps + 2)
                    pool.tensor_copy(dst[:, 1, :], src).then_inc(pool_step, 1)
                    hold(pool, pool_step, steps + 3)
                    pool.tensor_tensor(src, src, dst[:, 1, :], ALU.subtract).then_inc(pool_step, 1)
                    hold(pool, pool_step, steps + 4)
                    pool.tensor_copy(dst[:, 2, :], src).then_inc(parts_ready, 1)
                if not last:
                    hold(pool, slim_taken, (c + 1) * SLIM)
                    add_bias(c + 1)

            add_bias(0)
            chunks(pool, body)

        @block.vector
        def _(dve):
            def norm(c):
                base = c * DVE_STEPS
                hold(dve, x_in, 16 * (c + 1))
                for t in range(CT):
                    dve.bn_stats(stats[:, t, :], xt[:, t, :]).then_inc(dve_step, 1)
                hold(dve, dve_step, base + CT)
                for t in range(CT):
                    dve.bn_aggr(mv[:, t, :], stats[:, t, :]).then_inc(dve_step, 1)
                hold(dve, dve_step, base + 2 * CT)
                dve.tensor_scalar(var[:, :], mv[:, :, 1], EPS, None, ALU.add).then_inc(var_ready, 1)
                hold(dve, std_ready, c + 1)
                dve.reciprocal(rstd[:, :], std[:, :]).then_inc(dve_step, 1)
                hold(dve, dve_step, base + 2 * CT + 1)
                dve.tensor_tensor(newt[:, :], rstd[:, :], rstd[:, :], ALU.mult).then_inc(dve_step, 1)
                hold(dve, dve_step, base + 2 * CT + 2)
                dve.tensor_tensor(newt[:, :], newt[:, :], var[:, :], ALU.mult).then_inc(dve_step, 1)
                hold(dve, dve_step, base + 2 * CT + 3)
                dve.tensor_scalar(newt[:, :], newt[:, :], -0.5, 1.5, ALU.mult, ALU.add).then_inc(dve_step, 1)
                hold(dve, dve_step, base + 2 * CT + 4)
                dve.tensor_tensor(rstd[:, :], rstd[:, :], newt[:, :], ALU.mult).then_inc(dve_step, 1)
                hold(dve, dve_step, base + 2 * CT + 5)
                for t in range(CT):
                    last = dve.tensor_scalar(xn[:, t, :], xt[:, t, :], mv[:, t, 0:1], rstd[:, t:t + 1],
                                             ALU.subtract, ALU.mult)
                    if t == CT - 1:
                        last.then_inc(xn_ready, 1)
                hold(dve, xn_ready, c + 1)
                dve.sem_inc(x_used, 1)
                dve.sem_inc(dve_step, 1)

            def body(c, first, last):
                if not first:
                    hold(dve, v_out, 16 * c)
                for t in range(CT):
                    hold(dve, slim_ready, c * SLIM + t + 1)
                    dve.tensor_tensor(vt[:, :, t, 0:D],
                                      ps_slim[:, t % 2, 0:C].rearrange("p (h d) -> p h d", d=D),
                                      bvB[:, :].rearrange("p (h d) -> p h d", d=D), ALU.add)\
                       .then_inc(slim_taken, 1)
                if not last:
                    hold(dve, x_turned, c + 1)
                    norm(c + 1)
                hold(dve, xbo_ready, c + 2)
                if not first:
                    hold(dve, res_out, 16 * c)
                for t in range(CT):
                    hold(dve, slim_ready, c * SLIM + CT + t + 1)
                    dve.scalar_tensor_tensor(out=res[:, t, :], in0=ps_slim[:, t % 2, 0:C],
                                             scalar=scales[:, 2:3], in1=xbo[:, t, :],
                                             op0=ALU.mult, op1=ALU.add).then_inc(slim_taken, 1)

            norm(0)
            hold(dve, xbo_ready, 1)
            chunks(dve, body)

        @block.scalar
        def _(act):
            def root(c):
                act.wait_ge(var_ready, c + 1)
                act.activation(std[:, :], var[:, :], ACT.Sqrt).then_inc(std_ready, 1)

            def body(c, first, last):
                act.wait_ge(x_turned, c + 1)
                for kk in range(CK):
                    act.activation(xnT[:, kk, :], ps_x[:, kk, :], ACT.Copy).then_inc(xnT_ready, 1)
                for u in range(WIDE):
                    act.wait_ge(wide_ready, c * WIDE + u + 1)
                    src = ps_wide[:, u % 2, :]
                    if u < QK:
                        if not (first and u < 2):
                            act.wait_ge(parts_ready, c * QK + u - 1)
                        w, m = u // CK, u % CK
                        act.activation(piece[:, u % 2, :], src, ACT.Identity, bias=bqk[:, w, m:m + 1],
                                       scale=D ** -0.5 if w == 0 else 1.0).then_inc(wide_taken, 1)
                    else:
                        layer, m = (u - QK) // FK, (u - QK) % FK
                        dst = (h0, h1)[layer]
                        act.activation(dst[:, m, :], src, ACT.Relu, scale=scales[:, layer:layer + 1])\
                           .then_inc(wide_taken, 1)
                    if u == QK and not last:
                        root(c + 1)

            root(0)
            chunks(act, body)

        @block.tensor
        def _(pe):
            def body(c, first, last):
                pe.wait_ge(xn_ready, c + 1)
                if not first:
                    pe.wait_ge(xnT_ready, CK * c)
                for kk in range(CK):
                    for t in range(CT):
                        tr = pe.transpose(ps_x[:, kk, t * P:(t + 1) * P], xn[:, t, kk * P:(kk + 1) * P],
                                          ident[:, :])
                tr.then_inc(x_turned, 1)
                pe.wait_ge(xnT_ready, CK * (c + 1))

                def wide(u, k, lhs, rhs):
                    if not (first and u < 2):
                        pe.wait_ge(wide_taken, c * WIDE + u - 1)
                    for n in range(k):
                        mm = pe.matmul(ps_wide[:, u % 2, :], lhs(n), rhs(n), start=(n == 0), stop=(n == k - 1))
                    mm.then_inc(wide_ready, 1)

                def slim(u, k, lhs, rhs):
                    if not (first and u < 2):
                        pe.wait_ge(slim_taken, c * SLIM + u - 1)
                    for n in range(k):
                        mm = pe.matmul(ps_slim[:, u % 2, 0:C], lhs(n), rhs(n), start=(n == 0), stop=(n == k - 1))
                    mm.then_inc(slim_ready, 1)

                for u in range(QK):
                    w, m = u // CK, u % CK
                    wide(u, CK, lambda n: wT[:, w, n, m * P:(m + 1) * P], lambda n: xnT[:, n, :])
                for t in range(CT):
                    slim(t, CK, lambda n: xnT[:, n, t * P:(t + 1) * P], lambda n: wT[:, 2, n, :])
                for m in range(FK):
                    wide(QK + m, CK, lambda n: w0[:, n, m * P:(m + 1) * P], lambda n: xnT[:, n, :])
                pe.wait_ge(wide_taken, c * WIDE + QK + FK)
                for m in range(FK):
                    wide(QK + FK + m, FK, lambda n: w1[:, n, m * P:(m + 1) * P], lambda n: h0[:, n, :])
                pe.wait_ge(wide_taken, (c + 1) * WIDE)
                for t in range(CT):
                    slim(CT + t, FK, lambda n: h1[:, n, t * P:(t + 1) * P], lambda n: w2[:, n, :])

            chunks(pe, body)


def attend(nc, makers, g):
    sb, psum, sem = makers
    ident, flip, woT, out = (g[n] for n in ("ident", "flip", "woT", "out"))
    toep, q_parts, k_parts, v_pad, far_q, block_of_key, resid = (
        g[n] for n in ("toep", "q_parts", "k_parts", "v_pad", "far_q", "block_of_key", "resid"))
    B, T, C, KB, QUADS, TILES, BW = (g[n] for n in ("B", "T", "C", "KB", "QUADS", "TILES", "BW"))
    NQ = B * QUADS
    NT = NQ * TILES
    K_ROWS = QROWS + 3 * KB
    PV_LAG, OUT_LAG = 9, 11
    PE_PV, PE_OUT = 10, 12

    q_sb = sb("q_sb", [P, 2, HQ, T], BF16)
    k_sb = sb("k_sb", [P, 2, HQ, T], BF16)
    band = sb("band", [P, 2, HQ, 3, BW], BF16)
    v_sb = sb("v_sb", [P, HQ, KB, PD])
    s_sb = sb("s_sb", [P, 4, T])
    work = sb("work", [P, T])
    cand = sb("cand", [P, 4, 8 * (CHUNKS + 1)])
    rest = sb("rest", [P, 8 + 3 * CHUNKS])
    eighth = sb("eighth", [P, CHUNKS])
    unseen = sb("unseen", [P, 2])
    hides = sb("hides", [P, 2])
    hidden_sb = sb("hidden_sb", [1, 4])
    ones = sb("ones", [P, 1])
    e_sb = sb("e_sb", [P, 4, T])
    pT = sb("pT", [P, 2, HQ, KB, P])
    top = sb("top", [P, 4, TOPK])
    neg_max = sb("neg_max", [P, 4])
    den = sb("den", [P, 2, HQ])
    rden = sb("rden", [P, 2, HQ])
    rwide = sb("rwide", [P, HQ, PD])
    oT = sb("oT", [P, P])
    rT = sb("rT", [P, P])
    attnT = sb("attnT", [P, 2, P])
    y = sb("y", [P, 2, C])
    acc = sb("acc", [P, 2, KB, C])
    ps_s = psum("ps_s", [P, 2, T])
    ps_t = psum("ps_t", [P, 2, 512])
    ps_o = psum("ps_o2", [P, 512])
    ps_y = psum("ps_y", [P, 512])

    qkt_in = [sem("qkt_in0"), sem("qkt_in1")]
    v_in = sem("v_in")
    once_in = sem("once_in")
    acc_in = sem("acc_in")
    out_sent = sem("out_sent")
    s_ready = sem("s_ready")
    s_taken = sem("s_taken")
    top_step = sem("top_step")
    cand_ready = sem("cand_ready")
    exact_step = sem("exact_step")
    hides_ready = sem("hides_ready")
    hidden_ready = sem("hidden_ready")
    hidden_in = sem("hidden_in")
    ones_ready = sem("ones_ready")
    max_ready = sem("max_ready")
    neg_ready = sem("neg_ready")
    e_ready = sem("e_ready")
    p_ready = sem("p_ready")
    p_turned = sem("p_turned")
    pT_ready = sem("pT_ready")
    rden_ready = sem("rden_ready")
    rwide_ready = sem("rwide_ready")
    pv_ready = sem("pv_ready")
    pv_taken = sem("pv_taken")
    attn_ready = sem("attn_ready")
    y_ready = sem("y_ready")
    y_taken = sem("y_taken")
    acc_ready = sem("acc_ready")
    hold = holder(sem("tick2"))
    QKT = 16 * (2 * len(PAIRS) + 2)

    def quads(eng, body, lag):
        for i in range(TILES):
            body(0, i, True)
        with eng.Fori(1, NQ) as q:
            for i in range(TILES):
                body(q, i, False)
        if lag:
            for i in range(lag):
                body(NQ, i, False)

    with nc.Block() as block:

        @block.sync
        def _(sp):
            def load_qkt(b, hq, slot):
                h = HQ * hq
                sem_ = qkt_in[slot]
                for r, (a, c) in enumerate(PAIRS):
                    for dst, src, s in ((q_sb, q_parts, a), (k_sb, k_parts, c)):
                        sp.dma_start(dst[D * r:D * (r + 1), slot, :, :],
                                     src[b, s, h * D:(h + HQ) * D, :].rearrange("(j d) t -> d j t", d=D))\
                          .then_inc(sem_, 16)
                sp.dma_start(q_sb[QROWS:K_ROWS, slot, :, :],
                             far_q[:, :, h:h + HQ, :].rearrange("s r j t -> (s r) j t")).then_inc(sem_, 16)
                sp.dma_start(band[:, slot, :, :, :].rearrange("p j s c -> p j (s c)"),
                             toep[h:h + HQ].rearrange("h p c -> p h c")).then_inc(sem_, 16)

            def load_v(b, hq):
                sp.dma_start(v_sb[:, :, :, :].rearrange("p j k d -> p (j k d)"),
                             v_pad[b, :, HQ * hq:HQ * (hq + 1)].rearrange("p j k d -> p (j k d)"))\
                  .then_inc(v_in, 16)

            def load_acc(b, slot):
                sp.dma_start(acc[:, slot, :, :], resid[b].rearrange("(t p) e -> p t e", p=P)).then_inc(acc_in, 16)

            def send(b, slot):
                sp.wait_ge(acc_ready, (b + 1) * QUADS * KB)
                sp.dma_start(out[b].rearrange("(t p) e -> p t e", p=P), acc[:, slot, :, :]).then_inc(out_sent, 16)
                sp.wait_ge(out_sent, 16 * (b + 1))

            for s in range(3):
                sp.dma_start(k_sb[QROWS + KB * s:QROWS + KB * (s + 1), :, :, :].rearrange("r a j t -> r (a j) t"),
                             block_of_key.unsqueeze(1).broadcast_to([KB, 2 * HQ, T])).then_inc(once_in, 16)
            load_qkt(0, 0, 0)
            load_v(0, 0)
            load_acc(0, 0)
            load_qkt(0, 1, 1)

            def batch(b, first, last):
                for hq in range(QUADS):
                    n = b * QUADS + hq
                    if not (first and hq == 0):
                        sp.wait_ge(pv_ready, n * KB)
                        load_v(b, hq)
                        if not (last and hq == QUADS - 1):
                            sp.wait_ge(s_ready, n * TILES)
                            nh = (hq + 1) % QUADS
                            load_qkt(b + (1 if nh == 0 else 0), nh, nh % 2)
                    if hq == 1:
                        if not first:
                            send(b - 1, (b + 1) % 2)
                        if not last:
                            load_acc(b + 1, (b + 1) % 2)

            batch(0, True, False)
            with sp.Fori(1, B - 1) as b:
                batch(b, False, False)
            batch(B - 1, False, True)
            send(B - 1, (B - 1) % 2)

        @block.tensor
        def _(pe):
            def scores(q, i):
                qi, j, slot = i // HQ, i % HQ, q % 2
                t = q * TILES + i
                ps = ps_s[:, i % 2, :]
                near = range(max(qi - 3, 0), min(qi + 2, KB))
                for half in range(2):
                    blocks = [k for k in near if k // 4 == half]
                    mm = pe.matmul(ps[:, half * 512:(half + 1) * 512],
                                   q_sb[0:K_ROWS, slot, j, qi * P:(qi + 1) * P],
                                   k_sb[0:K_ROWS, slot, j, half * 512:(half + 1) * 512],
                                   start=True, stop=not blocks)
                    for s in range(3 if blocks else 0):
                        c = (blocks[0] - qi + 3) * P
                        w = len(blocks) * P
                        mm = pe.matmul(ps[:, blocks[0] * P:blocks[0] * P + w], flip[:, :],
                                       band[:, slot, j, s, c:c + w], start=False, stop=(s == 2))
                mm.then_inc(s_ready, 1)

            def turn(t, i):
                for half in range(2):
                    if not (isinstance(t, int) and t == 0):
                        pe.wait_ge(pT_ready, 2 * t - 1 + half)
                    for k in range(4 * half, 4 * half + 4):
                        tr = pe.transpose(ps_t[:, half, (k % 4) * P:(k % 4 + 1) * P],
                                          e_sb[:, i % 4, k * P:(k + 1) * P], ident[:, :])
                    tr.then_inc(p_turned, 1)

            def body(q, i, first):
                t = q * TILES + i
                over = isinstance(q, int) and q == NQ
                if not over:
                    if i == 0:
                        if first:
                            pe.wait_ge(once_in, 48)
                        if isinstance(q, int):
                            pe.wait_ge(qkt_in[q % 2], QKT * (q // 2 + 1))
                        else:
                            pe.wait_ge(qkt_in[0], QKT * ((q + 2) // 2))
                            pe.wait_ge(qkt_in[1], QKT * ((q + 1) // 2))
                    if not (first and i < 2):
                        pe.wait_ge(s_taken, t - 1)
                    scores(q, i)
                if not (first and i < 3) and not (over and i >= 3):
                    if first and i == 3:
                        pe.wait_ge(ones_ready, 1)
                    pe.wait_ge(hides_ready, t - 2)
                    if not (first and i < 4):
                        pe.wait_ge(hidden_in, t - 3)
                    if (i - 1) % HQ == PE_OUT % HQ and not (first and i <= PE_OUT):
                        pe.wait_ge(y_taken, q * KB + (i - 1 - PE_OUT) // HQ + 1)
                    pe.matmul(ps_y[0:1, C:C + 1], hides[:, (i - 3) % 2:(i - 3) % 2 + 1], ones[:, :],
                              start=True, stop=True).then_inc(hidden_ready, 1)
                if not (first and i < 5) and not (over and i >= 5):
                    pe.wait_ge(p_ready, t - 4)
                    turn(t - 5, i - 5)
                if i % HQ == PE_PV % HQ and not (first and i < PE_PV) and not (over and i >= PE_PV):
                    m = q * KB + (i - PE_PV) // HQ
                    mp = ((i - PE_PV) // HQ) % 2
                    if i == PE_PV:
                        pe.wait_ge(v_in, 16 * (q + 1))
                    pe.wait_ge(pT_ready, 2 * HQ * (m + 1))
                    if not (first and i == PE_PV):
                        pe.wait_ge(pv_taken, m)
                    for k in range(KB):
                        for j in range(HQ):
                            mm = pe.matmul(ps_o[PD * j:PD * (j + 1), 0:P], v_sb[:, j, k, :], pT[:, mp, j, k, :],
                                           start=(k == 0), stop=(k == KB - 1))
                    pe.wait_ge(rwide_ready, m + 1)
                    mm = pe.transpose(ps_o[:, P:2 * P], rwide[:, :, :].rearrange("p j d -> p (j d)"), ident[:, :])
                    mm.then_inc(pv_ready, 1)
                if i % HQ == PE_OUT % HQ and not (first and i < PE_OUT) and not (over and i >= PE_OUT):
                    m = q * KB + (i - PE_OUT) // HQ
                    mp = ((i - PE_OUT) // HQ) % 2
                    hq = q % QUADS if i >= PE_OUT else (q + QUADS - 1) % QUADS
                    pe.wait_ge(attn_ready, m + 1)
                    if not (over and i >= 3):
                        pe.wait_ge(hidden_in, t - 2)
                    pe.matmul(ps_y[:, 0:C], attnT[:, mp, :], woT[:, hq, :], start=True, stop=True)\
                      .then_inc(y_ready, 1)

            quads(pe, body, PE_OUT)

        @block.scalar
        def _(act):
            def body(q, i, first):
                t = q * TILES + i
                over = isinstance(q, int) and q == NQ
                if not over:
                    act.wait_ge(s_ready, t + 1)
                    if not (first and i < 4):
                        act.wait_ge(p_ready, t - 3)
                    act.activation(s_sb[:, i % 4, :], ps_s[:, i % 2, :], ACT.Copy).then_inc(s_taken, 1)
                if not (first and i < 2) and not (over and i >= 2):
                    act.wait_ge(neg_ready, t - 1)
                    if not (first and i < 6):
                        act.wait_ge(p_turned, 2 * (t - 5))
                    act.activation(e_sb[:, (i - 2) % 4, :], s_sb[:, (i - 2) % 4, :], ACT.Exp,
                                   bias=neg_max[:, (i - 2) % 4:(i - 2) % 4 + 1]).then_inc(e_ready, 1)
                if not (first and i < 4) and not (over and i >= 4):
                    mp, j = ((i - 4) // HQ) % 2, i % HQ
                    if not (first and i < 12):
                        act.wait_ge(pv_ready, q * KB + (i - 12) // HQ + 1)
                    for half in range(2):
                        act.wait_ge(p_turned, 2 * (t - 4) + 1 + half)
                        act.activation(pT[:, mp, j, 4 * half:4 * half + 4, :], ps_t[:, half, :], ACT.Copy)\
                           .then_inc(pT_ready, 1)
                if not (first and i < 2) and not (over and i >= 2):
                    act.wait_ge(hidden_ready, t - 1)
                    act.activation(hidden_sb[:, (i - 2) % 4:(i - 2) % 4 + 1], ps_y[0:1, C:C + 1], ACT.Copy)\
                       .then_inc(hidden_in, 1)
                if i % HQ == (PV_LAG + 1) % HQ and not (first and i < PV_LAG + 1) and not (over and i > PV_LAG):
                    m = q * KB + (i - PV_LAG - 1) // HQ
                    act.wait_ge(pv_ready, m + 1)
                    if not (first and i == PV_LAG + 1):
                        act.wait_ge(attn_ready, m)
                    act.activation(oT[:, :], ps_o[:, 0:P], ACT.Copy)
                    act.activation(rT[:, :], ps_o[:, P:2 * P], ACT.Copy).then_inc(pv_taken, 1)
                if i % HQ == OUT_LAG % HQ and not (first and i < OUT_LAG) and not (over and i >= OUT_LAG):
                    m = q * KB + (i - OUT_LAG) // HQ
                    act.wait_ge(y_ready, m + 1)
                    if not (first and i < OUT_LAG + 2 * HQ):
                        act.wait_ge(acc_ready, m - 1)
                    act.activation(y[:, ((i - OUT_LAG) // HQ) % 2, :], ps_y[:, 0:C], ACT.Copy)\
                       .then_inc(y_taken, 1)

            quads(act, body, OUT_LAG)

        @block.gpsimd
        def _(pool):
            pool.memset(ones[:, :], 1.0).then_inc(ones_ready, 1)

            def body(q, i, first):
                t = q * TILES + i
                over = isinstance(q, int) and q == NQ
                if not over:
                    hold(pool, max_ready, t + 1)
                    if not (first and i < 4):
                        hold(pool, e_ready, t - 3)
                    pool.tensor_scalar(neg_max[:, i % 4:i % 4 + 1], top[:, i % 4, 0:1], -1.0, None, ALU.mult)\
                        .then_inc(neg_ready, 1)
                if i % HQ == 0 and not (first and i < HQ):
                    m = q * KB + i // HQ - 1
                    if not (over and i > 0):
                        hold(pool, rden_ready, m + 1)
                        if not (first and i < 2 * HQ):
                            hold(pool, pv_ready, m)
                        pool.tensor_copy(rwide[:, :, :],
                                         rden[:, (i // HQ - 1) % 2, :].unsqueeze(2).broadcast_to([P, HQ, PD]))\
                            .then_inc(rwide_ready, 1)
                if i % HQ == (PV_LAG + 1) % HQ and not (first and i < PV_LAG + 1) and not (over and i > PV_LAG):
                    m = q * KB + (i - PV_LAG - 1) // HQ
                    mp = ((i - PV_LAG - 1) // HQ) % 2
                    hold(pool, pv_taken, m + 1)
                    if not (first and i < PV_LAG + 1 + 2 * HQ):
                        hold(pool, y_ready, m - 1)
                    pool.tensor_tensor(attnT[:, mp, :], oT[:, :], rT[:, :], ALU.mult).then_inc(attn_ready, 1)
                if i % HQ == (OUT_LAG + 1) % HQ and not (first and i < OUT_LAG + 1) and not (over and i > OUT_LAG):
                    m = q * KB + (i - OUT_LAG - 1) // HQ
                    tile = (i - OUT_LAG - 1) // HQ
                    batch = m // (KB * QUADS)
                    if tile % KB == 0:
                        hold(pool, acc_in, 16 * (batch + 1))
                    hold(pool, y_taken, m + 1)
                    a = acc[:, batch % 2, tile % KB, :]
                    pool.tensor_tensor(a, a, y[:, tile % 2, :], ALU.add).then_inc(acc_ready, 1)

            quads(pool, body, OUT_LAG + 1)

        @block.vector
        def _(dve):
            CHAIN = 2 * (TOPK // 8) - 1

            def part_of(s, c):
                n = (T // 4 - c + CHUNKS - 1) // CHUNKS
                return bass.AP(tensor=s.tensor, offset=s.offset + 4 * c, ap=[s.ap[0], [4 * CHUNKS, n], [1, 4]])

            def ranks(i, a, b):
                return cand[:, i % 4, 8 + (a - 1) * CHUNKS:8 + b * CHUNKS].rearrange("p (r c) -> p r c", c=CHUNKS)

            def exact(i):
                s, tp, w = s_sb[:, i % 4, :], top[:, i % 4, :], work[:, :]
                for n in range(1, TOPK // 8):
                    dve.match_replace(w, tp[:, 8 * n - 8:8 * n], s if n == 1 else w, NEG).then_inc(exact_step, 1)
                    dve.wait_ge(exact_step, 2 * n - 1)
                    dve.max(tp[:, 8 * n:8 * n + 8], w).then_inc(exact_step, 1)
                    if n < TOPK // 8 - 1:
                        dve.wait_ge(exact_step, 2 * n)
                dve.wait_ge(exact_step, CHAIN - 1)
                dve.sem_inc(exact_step, 1 - CHAIN)

            def body(q, i, first):
                t = q * TILES + i
                over = isinstance(q, int) and q == NQ
                chunks = iter([] if over else range(CHUNKS))
                picks = not (first and i < 1) and not (over and i >= 1)
                masks = not (first and i < 2)

                def fill(n):
                    for _ in range(n):
                        c = next(chunks, None)
                        if c is not None:
                            ins = dve.max(ranks(i, 1, 8)[:, :, c], part_of(s_sb[:, i % 4, :], c))
                            if c == 3 and picks:
                                ins.then_inc(max_ready, 1)
                            if c == CHUNKS - 1:
                                ins.then_inc(cand_ready, 1)

                if not over:
                    hold(dve, s_taken, t + 1)
                if picks:
                    tp = top[:, (i - 1) % 4, :]
                    src = cand[:, (i - 1) % 4, 0:8 + 3 * CHUNKS]
                    deep = cand[:, (i - 1) % 4, 0:8]
                    dve.wait_ge(cand_ready, 1)
                    dve.sem_inc(cand_ready, -1)
                    dve.max(deep, ranks(i - 1, 4, 7)).then_inc(top_step, 1)
                    fill(3)
                    dve.wait_ge(top_step, 1)
                    dve.max(tp[:, 0:8], src).then_inc(top_step, 1)
                    if over:
                        dve.wait_ge(top_step, 2)
                        dve.sem_inc(max_ready, 1)
                    else:
                        fill(3)
                    for n in range(1, TOPK // 8):
                        dve.wait_ge(top_step, 2 * n)
                        dve.match_replace(rest[:, :], tp[:, 8 * n - 8:8 * n], src if n == 1 else rest[:, :], NEG)\
                           .then_inc(top_step, 1)
                        fill(3)
                        dve.wait_ge(top_step, 2 * n + 1)
                        dve.max(tp[:, 8 * n:8 * n + 8], rest[:, :]).then_inc(top_step, 1)
                        fill(3 if n < TOPK // 8 - 1 else 0)
                    dve.tensor_scalar(eighth[:, :], ranks(i - 1, 8, 8), deep[:, 7:8], None, ALU.max, ALU.max,
                                      accum_out=unseen[:, (i - 1) % 2:(i - 1) % 2 + 1]).then_inc(top_step, 1)
                fill(CHUNKS)
                if masks:
                    hold(dve, hidden_in, t - 1)
                    hidden = dve.value_load(hidden_sb[0:1, (i - 2) % 4:(i - 2) % 4 + 1].bitcast(mybir.dt.int32))
                    with dve.If(hidden != 0):
                        exact(i - 2)
                    hold(dve, e_ready, t - 1)
                    e, s = e_sb[:, (i - 2) % 4, :], s_sb[:, (i - 2) % 4, :]
                    mp, j = ((i - 2) // HQ) % 2, (i - 2) % HQ
                    dve.scalar_tensor_tensor(out=e, in0=s, scalar=top[:, (i - 2) % 4, TOPK - 1:TOPK], in1=e,
                                             op0=ALU.is_ge, op1=ALU.mult, accum_out=den[:, mp, j:j + 1])\
                       .then_inc(p_ready, 1)
                if picks:
                    dve.wait_ge(top_step, CHAIN + 2)
                    dve.sem_inc(top_step, -(CHAIN + 2))
                    dve.tensor_tensor(hides[:, (i - 1) % 2:(i - 1) % 2 + 1], unseen[:, (i - 1) % 2:(i - 1) % 2 + 1],
                                      tp[:, TOPK - 1:TOPK], ALU.is_gt).then_inc(hides_ready, 1)
                if masks and j == HQ - 1:
                    m = q * KB + (i - 2) // HQ
                    hold(dve, p_ready, t - 1)
                    if not (first and i < 3 * HQ):
                        hold(dve, rwide_ready, m - 1)
                    dve.reciprocal(rden[:, mp, :], den[:, mp, :]).then_inc(rden_ready, 1)

            quads(dve, body, 2)


_INS = ["L0_attn_x", "L0_attn_Wq", "L0_attn_bq", "L0_attn_Wk", "L0_attn_bk", "L0_attn_Wv", "L0_attn_bv",
        "L0_attn_Wo", "L0_attn_bo", "L0_attn_head_gates", "L0_attn_rel_bias", "L0_ffn_k0", "L0_ffn_k1",
        "L0_ffn_k2", "L0_ffn_s0", "L0_ffn_s1", "L0_ffn_s2"]


def kernel(**inputs):
    import numpy as _np
    import concourse.bacc as _bacc
    from concourse import mybir as _mybir
    from concourse.bass_utils import run_bass_kernel_spmd as _run

    nc = _bacc.Bacc("TRN2", target_bir_lowering=False, num_devices=1)
    arrays, args = {}, []
    for name in _INS:
        a = _np.ascontiguousarray(inputs[name])
        a = a.reshape(a.shape or (1,))
        arrays[f"in_{name}_dram"] = a
        args.append(nc.dram_tensor(f"in_{name}_dram", a.shape, _mybir.dt.from_np(a.dtype), kind="ExternalInput").ap())
    out = nc.dram_tensor("out_0_dram", inputs["L0_attn_x"].shape, F32, kind="ExternalOutput").ap()
    attention_ffn_kernel(nc, *args, out)
    r = _run(nc, [arrays], core_ids=[0])
    return r.results[0]["out_0_dram"]
```

```python
from contextlib import ExitStack

import concourse.bass as bass
from concourse import mybir

F32 = mybir.dt.float32
BF16 = mybir.dt.bfloat16
U8 = mybir.dt.uint8
ALU = mybir.AluOpType
ACT = mybir.ActivationFunctionType

P = 128
H, D = 16, 16
TOPK = 32
MAXPOS = 128
EPS = 1e-5
NEG = -3.0e38
CHUNKS = 24
HQ = 4
PD = 32
BAND = 5
QROWS = 96
PAIRS = [(0, 0), (0, 1), (1, 0), (1, 1), (0, 2), (2, 0)]


def holder(tick):
    def hold(eng, sem, value):
        eng.wait_ge(sem, value)
        if not isinstance(value, int):
            eng.sem_inc(tick, 1)
    return hold


def attention_ffn_kernel(nc, x, Wq, bq, Wk, bk, Wv, bv, Wo, bo, gates, rel, k0, k1, k2, s0, s1, s2, out):
    B, T, C = x.shape
    F0, F1 = k0.shape[1], k1.shape[1]
    KB = T // P
    NCH = B * 2
    CH = T // 2
    CT = CH // P
    CK = C // P
    QUADS = H // HQ
    TILES = KB * HQ
    BW = BAND * P
    FV = T // 2 + 2 * P
    assert CK == 2 and H * D == C and F0 == 1024 and F1 == 1024

    fvec = nc.dram_tensor("fvec", [H, FV], F32).ap()
    toep = nc.dram_tensor("toep", [H, P, 3 * BW], BF16).ap()
    q_parts = nc.dram_tensor("q_parts", [B, 3, C, T], BF16).ap()
    k_parts = nc.dram_tensor("k_parts", [B, 3, C, T], BF16).ap()
    v_all = nc.dram_tensor("v_all", [B, P, H, KB, D], F32).ap()
    far_q = nc.dram_tensor("far_q", [3, KB, H, T], BF16).ap()
    block_of_key = nc.dram_tensor("block_of_key", [KB, T], BF16).ap()
    x_parts = nc.dram_tensor("x_parts", [B, P, CK, 3, T], BF16).ap()

    nc.disable_value_cache = True
    with ExitStack() as whole:
        def tensors(ctx):
            return (lambda n, s, d=F32: ctx.enter_context(nc.sbuf_tensor(n, s, d)),
                    lambda n, s, d=F32: ctx.enter_context(nc.psum_tensor(n, s, d)),
                    lambda n: ctx.enter_context(nc.semaphore(n)))

        sb, _, _ = tensors(whole)
        ident = sb("ident", [P, P])
        flip = sb("flip", [P, P], BF16)
        woT = sb("woT", [P, QUADS, C])
        w0 = sb("w0", [P, CK, F0], BF16)
        w1 = sb("w1", [P, F0 // P, F1], BF16)
        w2 = sb("w2", [P, F1 // P, C], BF16)
        scales = sb("scales", [P, 3])
        with ExitStack() as early:
            sbe, _, _ = tensors(early)
            wT = sbe("wT", [P, 3, CK, C])
            bqk = sbe("bqk", [P, 2, CK])
            bvB = sbe("bvB", [P, C])
            boB = sbe("boB", [P, C])
            with ExitStack() as ctx:
                setup(nc, tensors(ctx), locals())
            with ExitStack() as ctx:
                project(nc, tensors(ctx), locals())
        with ExitStack() as ctx:
            attend(nc, tensors(ctx), locals())


def setup(nc, makers, g):
    sb, psum, sem = makers
    x, Wq, bq, Wk, bk, Wv, bv, Wo, bo = (g[n] for n in ("x", "Wq", "bq", "Wk", "bk", "Wv", "bv", "Wo", "bo"))
    gates, rel, k0, k1, k2, s0, s1, s2 = (g[n] for n in ("gates", "rel", "k0", "k1", "k2", "s0", "s1", "s2"))
    ident, flip, woT, wT, w0, w1, w2 = (g[n] for n in ("ident", "flip", "woT", "wT", "w0", "w1", "w2"))
    bqk, bvB, boB, scales = (g[n] for n in ("bqk", "bvB", "boB", "scales"))
    fvec, toep, far_q, block_of_key = (g[n] for n in ("fvec", "toep", "far_q", "block_of_key"))
    C, T, KB, CK, QUADS, BW, FV = (g[n] for n in ("C", "T", "KB", "CK", "QUADS", "BW", "FV"))
    NR = 2 * MAXPOS - 1

    w_nat = sb("w_nat", [P, 4, CK, C])
    kb0 = sb("kb0", [P, 2 * CK, 1024], U8)
    kb1 = sb("kb1", [P, 8, 1024], U8)
    kb2 = sb("kb2", [P, 8, C], U8)
    gateB = sb("gateB", [P, H])
    wo_pad = sb("wo_pad", [P, CK, H, PD])
    relT = sb("relT", [H, NR])
    fv = sb("fv", [H, FV])
    far = sb("far", [KB, 2, H])
    m_lo = sb("m_lo", [KB, KB])
    m_hi = sb("m_hi", [KB, KB])
    f_a = sb("f_a", [KB, H, KB])
    f_b = sb("f_b", [KB, H, KB])
    f_part = sb("f_part", [KB, 3, H, KB], BF16)
    f_wide = sb("f_wide", [KB, H, KB, P], BF16)
    onehot = sb("onehot", [KB, KB, P], BF16)
    t_f = sb("t_f", [P, 4, BW])
    t_part = sb("t_part", [P, 4, 3, BW], BF16)
    ps_w = psum("ps_w", [P, 3, CK, C])
    ps_o = psum("ps_o", [P, QUADS, C])

    loaded = sem("loaded")
    rel_loaded = sem("rel_loaded")
    table_done = sem("table_done")
    table_out = sem("table_out")
    band_in = sem("band_in")
    band_done = sem("band_done")
    band_out = sem("band_out")
    far_done = sem("far_done")
    far_out = sem("far_out")
    ident_done = sem("ident_done")
    pool_step = sem("pool_step")
    dve_step = sem("dve_step")
    wo_ready = sem("wo_ready")
    turned = sem("turned")
    LOADS = 15 * 16

    with nc.Block() as block:

        @block.sync
        def _(sp):
            with nc.allow_non_contiguous_dma("short vectors"):
                sp.dma_start(relT[:, :], rel.rearrange("r h -> h r")).then_inc(rel_loaded, 16)
                sp.dma_start(far[:, 0, :], rel[0, :].partition_broadcast(KB)).then_inc(rel_loaded, 16)
                sp.dma_start(far[:, 1, :], rel[NR - 1, :].partition_broadcast(KB)).then_inc(rel_loaded, 16)
                for n, w in enumerate((Wq, Wk, Wv, Wo)):
                    sp.dma_start(w_nat[:, n, :, :], w.rearrange("(o p) i -> p o i", p=P)).then_inc(loaded, 16)
                for dst, src in ((kb0, k0), (kb1, k1), (kb2, k2)):
                    sp.dma_start(dst[:, :, :], src.rearrange("(k p) n -> p k n", p=P)).then_inc(loaded, 16)
                for n, b in enumerate((bq, bk)):
                    sp.dma_start(bqk[:, n, :], b.rearrange("(m p) -> p m", p=P)).then_inc(loaded, 16)
                sp.dma_start(bvB[:, :], bv.partition_broadcast(P)).then_inc(loaded, 16)
                sp.dma_start(boB[:, :], bo.partition_broadcast(P)).then_inc(loaded, 16)
                sp.dma_start(gateB[:, :], gates.partition_broadcast(P)).then_inc(loaded, 16)
                for n, s in enumerate((s0, s1, s2)):
                    sp.dma_start(scales[:, n:n + 1], s.partition_broadcast(P)).then_inc(loaded, 16)
            sp.wait_ge(table_done, 1)
            sp.dma_start(fvec, fv[:, :]).then_inc(table_out, 16)
            sp.wait_ge(table_out, 16)
            for n in range(H // 4):
                if n:
                    sp.wait_ge(band_done, n)
                for h in range(4 * n, 4 * n + 4):
                    src = bass.AP(tensor=fvec.tensor, offset=h * FV, ap=[[1, P], [1, BW]])
                    sp.dma_start(t_f[:, h % 4, :], src).then_inc(band_in, 16)
                sp.wait_ge(band_done, n + 1)
                sp.dma_start(toep[4 * n:4 * n + 4].rearrange("h p c -> p h c"),
                             t_part[:, :, :, :].rearrange("p h s c -> p h (s c)")).then_inc(band_out, 16)
            sp.wait_ge(ident_done, 3)
            sp.dma_start(block_of_key, onehot[:, :, :].rearrange("r b c -> r (b c)")).then_inc(far_out, 16)
            for s in range(3):
                sp.wait_ge(far_done, s + 1)
                sp.dma_start(far_q[s], f_wide[:, :, :, :].rearrange("r h i c -> r h (i c)")).then_inc(far_out, 16)
            sp.wait_ge(far_out, 64)
            sp.wait_ge(band_out, 16 * (H // 4))

        @block.gpsimd
        def _(pool):
            def link(ins, count=[0]):
                count[0] += 1
                ins.then_inc(pool_step, 1)
                pool.wait_ge(pool_step, count[0])

            link(pool.memset(ident[:, :], 0.0))
            pool.affine_select(out=ident[:, :], in_=ident[:, :], compare_op=ALU.not_equal, fill=1.0,
                               base=0, pattern=[[-1, P]], channel_multiplier=1).then_inc(ident_done, 1)
            link(pool.memset(flip[:, :], 0.0))
            pool.affine_select(out=flip[:, :], in_=flip[:, :], compare_op=ALU.not_equal, fill=1.0,
                               base=1 - P, pattern=[[1, P]], channel_multiplier=1)
            link(pool.memset(onehot[:, :, :], 1.0))
            pool.affine_select(out=onehot[:, :, :], in_=onehot[:, :, :], compare_op=ALU.is_equal, fill=0.0,
                               base=0, pattern=[[-1, KB], [0, P]], channel_multiplier=1).then_inc(ident_done, 1)
            link(pool.memset(m_lo[:, :], 1.0))
            link(pool.memset(m_hi[:, :], 1.0))
            link(pool.affine_select(out=m_lo[:, :], in_=m_lo[:, :], compare_op=ALU.is_ge, fill=0.0,
                                    base=-4, pattern=[[1, KB]], channel_multiplier=-1))
            pool.affine_select(out=m_hi[:, :], in_=m_hi[:, :], compare_op=ALU.is_ge, fill=0.0,
                               base=-2, pattern=[[-1, KB]], channel_multiplier=1).then_inc(ident_done, 1)

        @block.vector
        def _(dve):
            def link(ins, count=[0]):
                count[0] += 1
                ins.then_inc(dve_step, 1)
                dve.wait_ge(dve_step, count[0])

            def parts(dst, src):
                link(dve.tensor_copy(dst(0), src))
                link(dve.tensor_tensor(src, src, dst(0), ALU.subtract))
                link(dve.tensor_copy(dst(1), src))
                link(dve.tensor_tensor(src, src, dst(1), ALU.subtract))
                return dve.tensor_copy(dst(2), src)

            dve.wait_ge(rel_loaded, 48)
            a = FV - 1 - P - 2 * NR
            dve.tensor_copy(fv[:, 0:a], relT[:, 0:1].broadcast_to([H, a]))
            dve.tensor_copy(fv[:, a:a + NR], relT[:, :])
            dve.tensor_copy(fv[:, a + NR:a + 2 * NR], relT[:, :])
            dve.tensor_copy(fv[:, a + 2 * NR:FV], relT[:, NR - 1:NR].broadcast_to([H, FV - a - 2 * NR]))\
               .then_inc(table_done, 1)
            dve.wait_ge(loaded, LOADS)
            link(dve.memset(wo_pad[:, :, :, :], 0.0))
            for o in range(CK):
                dve.tensor_tensor(wo_pad[:, o, :, 0:D], w_nat[:, 3, o, :].rearrange("p (h d) -> p h d", d=D),
                                  gateB[:, :].unsqueeze(2).broadcast_to([P, H, D]), ALU.mult)\
                   .then_inc(wo_ready, 1)
            dve.tensor_tensor(w0[:, :, :], kb0[:, 0:CK, :], kb0[:, CK:2 * CK, :], ALU.subtract)
            for dst, src in ((w1, kb1), (w2, kb2)):
                dve.tensor_scalar(dst[:, :, :], src[:, :, :], 2.0, -1.0, ALU.mult, ALU.add)
            dve.tensor_scalar(scales[:, 0:1], scales[:, 0:1], 4.0, None, ALU.mult)
            dve.tensor_scalar(scales[:, 1:2], scales[:, 1:2], 2.0, None, ALU.mult)
            dve.tensor_scalar(bqk[:, 0, :], bqk[:, 0, :], D ** -0.5, None, ALU.mult)
            for n in range(H // 4):
                dve.wait_ge(band_in, 64 * (n + 1))
                if n:
                    dve.wait_ge(band_out, 16 * n)
                parts(lambda s: t_part[:, :, s, :], t_f[:, :, :]).then_inc(band_done, 1)
            dve.wait_ge(ident_done, 3)
            lo = far[:, 0, :].unsqueeze(2).broadcast_to([KB, H, KB])
            hi = far[:, 1, :].unsqueeze(2).broadcast_to([KB, H, KB])
            link(dve.tensor_tensor(f_a[:, :, :], lo, m_lo[:, :].unsqueeze(1).broadcast_to([KB, H, KB]), ALU.mult))
            link(dve.tensor_tensor(f_b[:, :, :], hi, m_hi[:, :].unsqueeze(1).broadcast_to([KB, H, KB]), ALU.mult))
            link(dve.tensor_tensor(f_a[:, :, :], f_a[:, :, :], f_b[:, :, :], ALU.add))
            link(parts(lambda s: f_part[:, s, :, :], f_a[:, :, :]))
            for s in range(3):
                if s:
                    dve.wait_ge(far_out, 16 * (s + 1))
                dve.tensor_copy(f_wide[:, :, :, :],
                                f_part[:, s, :, :].unsqueeze(3).broadcast_to([KB, H, KB, P]))\
                   .then_inc(far_done, 1)

        @block.tensor
        def _(pe):
            pe.wait_ge(loaded, LOADS)
            pe.wait_ge(ident_done, 1)
            for w in range(3):
                for kk in range(CK):
                    for o in range(CK):
                        last = pe.transpose(ps_w[:, w, kk, o * P:(o + 1) * P],
                                            w_nat[:, w, o, kk * P:(kk + 1) * P], ident[:, :])
            last.then_inc(turned, 1)
            pe.wait_ge(wo_ready, CK)
            for q in range(QUADS):
                for o in range(CK):
                    last = pe.transpose(ps_o[:, q, o * P:(o + 1) * P],
                                        wo_pad[:, o, q * HQ:(q + 1) * HQ, :].rearrange("p h d -> p (h d)"),
                                        ident[:, :])
            last.then_inc(turned, 1)

        @block.scalar
        def _(act):
            act.wait_ge(turned, 1)
            for w in range(3):
                act.activation(wT[:, w, :, :], ps_w[:, w, :, :], ACT.Copy)
            act.wait_ge(turned, 2)
            for q in range(QUADS):
                act.activation(woT[:, q, :], ps_o[:, q, :], ACT.Copy)


def project(nc, makers, g):
    sb, psum, sem = makers
    x, out, ident, wT, bqk, bvB, boB = (g[n] for n in ("x", "out", "ident", "wT", "bqk", "bvB", "boB"))
    x_parts, q_parts, k_parts, v_all = (g[n] for n in ("x_parts", "q_parts", "k_parts", "v_all"))
    C, CK, CT, CH, NCH = (g[n] for n in ("C", "CK", "CT", "CH", "NCH"))
    QK = 2 * CK
    NP = CK + QK
    POOLS = 3

    xt = sb("xt", [P, CT, C])
    xbo = sb("xbo", [P, CT, C])
    xn = sb("xn", [P, CT, C])
    stats = sb("stats", [P, CT, 6])
    mv = sb("mv", [P, CT, 2])
    var = sb("var", [P, CT])
    std = sb("std", [P, CT])
    rstd = sb("rstd", [P, CT])
    newt = sb("newt", [P, CT])
    xnT = sb("xnT", [P, CK, CH])
    piece = sb("piece", [P, QK, CH])
    part = sb("part", [P, NP, 3, CH], BF16)
    left = sb("left", [P, NP, CH])
    vt = sb("vt", [P, H, CT, D])
    ps_x = psum("ps_x", [P, CK, CH])
    ps_wide = psum("ps_wide", [P, QK, CH])
    ps_slim = psum("ps_slim", [P, 2, 512])

    x_in = sem("x_in")
    x_used = sem("x_used")
    var_ready = sem("var_ready")
    std_ready = sem("std_ready")
    xn_ready = sem("xn_ready")
    norm_step = sem("norm_step")
    xbo_ready = sem("xbo_ready")
    x_turned = sem("x_turned")
    xnT_ready = sem("xnT_ready")
    first_ready = sem("first_ready")
    wide_ready = sem("wide_ready")
    wide_taken = sem("wide_taken")
    slim_ready = sem("slim_ready")
    slim_taken = sem("slim_taken")
    pool_parts = sem("pool_parts")
    dve_parts = sem("dve_parts")
    pool_step = sem("pool_step2")
    dve_step = sem("dve_step2")
    parts_out = [sem(f"parts_out{n}") for n in range(NP)]
    v_out = sem("v_out")
    res_out = sem("res_out")
    hold = holder(sem("tick"))
    DVE_STEPS = CT + CT + 5 + 1

    def chunks(eng, body):
        body(0, True, 2)
        with eng.Fori(1, NCH - 2) as c:
            body(c, False, 2)
        body(NCH - 2, False, 1)
        body(NCH - 1, False, 0)

    def split(eng, n, step, done):
        src = xnT[:, n, :] if n < CK else piece[:, n - CK, :]
        rest = left[:, n, :]
        eng.tensor_tensor(part[:, n, 1, :], src, part[:, n, 0, :], ALU.subtract)
        eng.tensor_tensor(rest, src, part[:, n, 0, :], ALU.subtract).then_inc(step, 1)
        eng.wait_ge(step, 1)
        eng.sem_inc(step, -1)
        eng.tensor_tensor(part[:, n, 2, :], rest, part[:, n, 1, :], ALU.subtract).then_inc(done, 1)

    with nc.Block() as block:

        @block.sync
        def _(sp):
            def half(a, c):
                return a[c // 2].rearrange("(h t p) e -> h p t e", p=P, h=2)[c % 2]

            def load_x(c):
                sp.dma_start(xt[:, :, :], half(x, c)).then_inc(x_in, 16)

            def store_xbo(c):
                sp.wait_ge(xbo_ready, c + 1)
                sp.dma_start(half(out, c), xbo[:, :, :]).then_inc(res_out, 16)

            def store_part(c, n):
                if n < POOLS:
                    sp.wait_ge(pool_parts, c * POOLS + n + 1)
                else:
                    sp.wait_ge(dve_parts, c * (NP - POOLS) + n - POOLS + 1)
                if n < CK:
                    dst = x_parts[c // 2].rearrange("p k s (h t) -> h k p s t", h=2)[c % 2, n]
                else:
                    dst = (q_parts if n < 2 * CK else k_parts)[c // 2].rearrange(
                        "s (m p) (h t) -> h m p s t", p=P, h=2)[c % 2, n % CK]
                sp.dma_start(dst, part[:, n, :, :]).then_inc(parts_out[n], 16)

            def body(c, first, ahead):
                if ahead >= 1:
                    store_xbo(c + 1)
                if ahead >= 2:
                    sp.wait_ge(x_used, 2 * (c + 2))
                    load_x(c + 2)
                for n in range(POOLS):
                    store_part(c, n)
                sp.wait_ge(slim_taken, (c + 1) * CT)
                sp.dma_start(v_all[c // 2].rearrange("p h (f k) d -> f p h (k d)", f=2)[c % 2],
                             vt[:, :, :, :].rearrange("p h k d -> p h (k d)")).then_inc(v_out, 16)
                for n in range(POOLS, NP):
                    store_part(c, n)

            load_x(0)
            store_xbo(0)
            sp.wait_ge(x_used, 2)
            load_x(1)
            chunks(sp, body)
            for n in range(NP):
                sp.wait_ge(parts_out[n], 16 * NCH)
            sp.wait_ge(v_out, 16 * NCH)
            sp.wait_ge(res_out, 16 * NCH)

        @block.gpsimd
        def _(pool):
            def add_bias(c, first):
                hold(pool, x_in, 16 * (c + 1))
                if not first:
                    hold(pool, res_out, 16 * c)
                pool.tensor_tensor(xbo[:, :, :], xt[:, :, :],
                                   boB[:, :].unsqueeze(1).broadcast_to([P, CT, C]), ALU.add)\
                    .then_inc(xbo_ready, 1)
                hold(pool, xbo_ready, c + 1)
                pool.sem_inc(x_used, 1)

            def body(c, first, ahead):
                if ahead:
                    add_bias(c + 1, False)
                for n in range(POOLS):
                    if n < CK:
                        hold(pool, first_ready, CK * c + n + 1)
                    else:
                        hold(pool, wide_taken, QK * c + n - CK + 1)
                    split(pool, n, pool_step, pool_parts)

            add_bias(0, True)
            chunks(pool, body)

        @block.vector
        def _(dve):
            def norm(c):
                base = c * DVE_STEPS
                hold(dve, x_in, 16 * (c + 1))
                for t in range(CT):
                    dve.bn_stats(stats[:, t, :], xt[:, t, :]).then_inc(norm_step, 1)
                hold(dve, norm_step, base + CT)
                for t in range(CT):
                    dve.bn_aggr(mv[:, t, :], stats[:, t, :]).then_inc(norm_step, 1)
                hold(dve, norm_step, base + 2 * CT)
                dve.tensor_scalar(var[:, :], mv[:, :, 1], EPS, None, ALU.add).then_inc(var_ready, 1)
                hold(dve, std_ready, c + 1)
                dve.reciprocal(rstd[:, :], std[:, :]).then_inc(norm_step, 1)
                hold(dve, norm_step, base + 2 * CT + 1)
                dve.tensor_tensor(newt[:, :], rstd[:, :], rstd[:, :], ALU.mult).then_inc(norm_step, 1)
                hold(dve, norm_step, base + 2 * CT + 2)
                dve.tensor_tensor(newt[:, :], newt[:, :], var[:, :], ALU.mult).then_inc(norm_step, 1)
                hold(dve, norm_step, base + 2 * CT + 3)
                dve.tensor_scalar(newt[:, :], newt[:, :], -0.5, 1.5, ALU.mult, ALU.add).then_inc(norm_step, 1)
                hold(dve, norm_step, base + 2 * CT + 4)
                dve.tensor_tensor(rstd[:, :], rstd[:, :], newt[:, :], ALU.mult).then_inc(norm_step, 1)
                hold(dve, norm_step, base + 2 * CT + 5)
                for t in range(CT):
                    last = dve.tensor_scalar(xn[:, t, :], xt[:, t, :], mv[:, t, 0:1], rstd[:, t:t + 1],
                                             ALU.subtract, ALU.mult)
                    if t == CT - 1:
                        last.then_inc(xn_ready, 1)
                hold(dve, xn_ready, c + 1)
                dve.sem_inc(x_used, 1)
                dve.sem_inc(norm_step, 1)

            def body(c, first, ahead):
                if ahead:
                    hold(dve, x_turned, c + 1)
                    norm(c + 1)
                if not first:
                    hold(dve, v_out, 16 * c)
                for t in range(CT):
                    hold(dve, slim_ready, c * CT + t + 1)
                    dve.tensor_tensor(vt[:, :, t, :],
                                      ps_slim[:, t % 2, 0:C].rearrange("p (h d) -> p h d", d=D),
                                      bvB[:, :].rearrange("p (h d) -> p h d", d=D), ALU.add)\
                       .then_inc(slim_taken, 1)
                for n in range(POOLS, NP):
                    hold(dve, wide_taken, QK * c + n - CK + 1)
                    split(dve, n, dve_step, dve_parts)

            norm(0)
            chunks(dve, body)

        @block.scalar
        def _(act):
            def root(c):
                act.wait_ge(var_ready, c + 1)
                act.activation(std[:, :], var[:, :], ACT.Sqrt).then_inc(std_ready, 1)

            def body(c, first, ahead):
                act.wait_ge(x_turned, c + 1)
                for kk in range(CK):
                    if not first:
                        act.wait_ge(pool_parts, (c - 1) * POOLS + kk + 1)
                    act.activation(xnT[:, kk, :], ps_x[:, kk, :], ACT.Copy).then_inc(xnT_ready, 1)
                for kk in range(CK):
                    if not first:
                        act.wait_ge(parts_out[kk], 16 * c)
                    act.activation(part[:, kk, 0, :], ps_x[:, kk, :], ACT.Copy).then_inc(first_ready, 1)
                if ahead:
                    root(c + 1)
                for u in range(QK):
                    act.wait_ge(wide_ready, c * QK + u + 1)
                    n = CK + u
                    if not first:
                        if n < POOLS:
                            act.wait_ge(pool_parts, (c - 1) * POOLS + n + 1)
                        else:
                            act.wait_ge(dve_parts, (c - 1) * (NP - POOLS) + n - POOLS + 1)
                    w, m = u // CK, u % CK
                    form = dict(bias=bqk[:, w, m:m + 1], scale=D ** -0.5 if w == 0 else 1.0)
                    act.activation(piece[:, u, :], ps_wide[:, u, :], ACT.Identity, **form)
                    if not first:
                        act.wait_ge(parts_out[n], 16 * c)
                    act.activation(part[:, n, 0, :], ps_wide[:, u, :], ACT.Identity, **form)\
                       .then_inc(wide_taken, 1)

            root(0)
            chunks(act, body)

        @block.tensor
        def _(pe):
            def body(c, first, ahead):
                pe.wait_ge(xn_ready, c + 1)
                if not first:
                    pe.wait_ge(first_ready, CK * c)
                for kk in range(CK):
                    for t in range(CT):
                        tr = pe.transpose(ps_x[:, kk, t * P:(t + 1) * P], xn[:, t, kk * P:(kk + 1) * P],
                                          ident[:, :])
                tr.then_inc(x_turned, 1)
                pe.wait_ge(xnT_ready, CK * (c + 1))
                for u in range(QK):
                    w, m = u // CK, u % CK
                    if not first:
                        pe.wait_ge(wide_taken, (c - 1) * QK + u + 1)
                    for n in range(CK):
                        mm = pe.matmul(ps_wide[:, u, :], wT[:, w, n, m * P:(m + 1) * P], xnT[:, n, :],
                                       start=(n == 0), stop=(n == CK - 1))
                    mm.then_inc(wide_ready, 1)
                for t in range(CT):
                    if not (first and t < 2):
                        pe.wait_ge(slim_taken, c * CT + t - 1)
                    for n in range(CK):
                        mm = pe.matmul(ps_slim[:, t % 2, 0:C], xnT[:, n, t * P:(t + 1) * P], wT[:, 2, n, :],
                                       start=(n == 0), stop=(n == CK - 1))
                    mm.then_inc(slim_ready, 1)

            chunks(pe, body)


def attend(nc, makers, g):
    sb, psum, sem = makers
    ident, flip, woT, out = (g[n] for n in ("ident", "flip", "woT", "out"))
    w0, w1, w2, scales = (g[n] for n in ("w0", "w1", "w2", "scales"))
    toep, x_parts, q_parts, k_parts, v_all, far_q, block_of_key = (
        g[n] for n in ("toep", "x_parts", "q_parts", "k_parts", "v_all", "far_q", "block_of_key"))
    B, T, C, KB, QUADS, TILES, BW = (g[n] for n in ("B", "T", "C", "KB", "QUADS", "TILES", "BW"))
    NQ = B * QUADS
    NT = NQ * TILES
    FT = T // QUADS
    MT = w1.shape[1]
    UNITS = MT // 2 * 2 + 1
    HU = UNITS - 1
    PARTS = 3 * 2
    plan = [(u, 0, PARTS * C // P) for u in range(MT // 2)]
    for n, u in enumerate(range(MT // 2, UNITS)):
        left = (TILES - len(plan)) // (UNITS - u) if n >= 3 else -(-(TILES - len(plan)) // (UNITS - u))
        cuts = [PARTS * MT * c // left for c in range(left + 1)]
        plan += [(u, a, b) for a, b in zip(cuts, cuts[1:])]
    assert len(plan) == TILES and plan[-1][0] == HU

    K_ROWS = QROWS + 3 * KB
    RDEN, RWIDE, PV, PV_COPY, OUT, OUT_COPY, OUT_ADD = 9, 9, 9, 11, 14, 13, 14

    q_sb = sb("q_sb", [P, 2, HQ, T], BF16)
    k_sb = sb("k_sb", [P, 2, HQ, T], BF16)
    band = sb("band", [P, HQ, 3, BW], BF16)
    v_next = sb("v_next", [P, HQ, KB, D])
    v_sb = sb("v_sb", [P, HQ, KB, D])
    s_sb = sb("s_sb", [P, 4, T])
    work = sb("work", [P, T])
    cand = sb("cand", [P, 2, 8 * (CHUNKS + 1)])
    kept = sb("kept", [P, 2, T], BF16)
    rest = sb("rest", [P, 8 + 3 * CHUNKS])
    eighth = sb("eighth", [P, CHUNKS])
    unseen = sb("unseen", [P, 2])
    hides = sb("hides", [P, 2])
    hidden_sb = sb("hidden_sb", [1, 4])
    ones = sb("ones", [P, 1])
    e_sb = sb("e_sb", [P, 4, T])
    pT = sb("pT", [P, 2, HQ, KB, P])
    top = sb("top", [P, 4, TOPK])
    neg_max = sb("neg_max", [P, 4])
    den = sb("den", [P, 2, HQ])
    rden = sb("rden", [P, 2, HQ])
    rwide = sb("rwide", [P, HQ, PD])
    orT = sb("orT", [P, 2, P])
    attnT = sb("attnT", [P, 2, P])
    y = sb("y", [P, 2, C])
    acc = sb("acc", [P, 2, KB, C])
    ps_s = psum("ps_s", [P, 2, T])
    ps_t = psum("ps_t", [P, 2, 512])
    ps_o = psum("ps_o2", [P, 512])
    ps_f = psum("ps_f", [P, 2, FT])
    yc = 2 * P
    xp = sb("xp", [P, C // P, 3, FT], BF16)
    h0 = sb("h0", [P, MT, 3, FT], BF16)
    h1 = sb("h1", [P, MT, 3, FT], BF16)
    hf = sb("hf", [P, 2, 2, FT])

    qk_in = sem("qk_in")
    band_in = sem("band_in2")
    xp_in = sem("xp_in")
    ffn_ready = sem("ffn_ready")
    ffn_taken = sem("ffn_taken")
    split_step = sem("split_step")
    h_ready = sem("h_ready")
    acc_f = sem("acc_f")
    v_in = sem("v_in")
    v_ready = sem("v_ready")
    o_cleared = sem("o_cleared")
    once_in = sem("once_in")
    acc_in = sem("acc_in")
    out_sent = sem("out_sent")
    s_ready = sem("s_ready")
    s_taken = sem("s_taken")
    top_step = sem("top_step")
    cand_ready = sem("cand_ready")
    exact_step = sem("exact_step")
    hides_ready = sem("hides_ready")
    hidden_ready = sem("hidden_ready")
    hidden_in = sem("hidden_in")
    ones_ready = sem("ones_ready")
    max_ready = sem("max_ready")
    neg_ready = sem("neg_ready")
    e_ready = sem("e_ready")
    p_dve = sem("p_dve")
    p_pool = sem("p_pool")
    checked = sem("checked")
    kept_step = sem("kept_step")
    summed = sem("summed")
    p_turned = sem("p_turned")
    pT_ready = sem("pT_ready")
    rden_ready = sem("rden_ready")
    rwide_ready = sem("rwide_ready")
    pv_ready = sem("pv_ready")
    pv_taken = sem("pv_taken")
    attn_ready = sem("attn_ready")
    y_ready = sem("y_ready")
    y_taken = sem("y_taken")
    acc_y = sem("acc_y")
    hold = holder(sem("tick2"))
    QK_IN = 16 * (2 * len(PAIRS) + 1)

    def in_group(q, i, lag):
        return q * KB + (i - lag) // HQ if (i - lag) % HQ == 0 else None

    def masked(q, i):
        return (p_pool if i % 2 else p_dve), halves(q, i) + 1

    def halves(q, i):
        return q * (TILES // 2) + i // 2

    def ended_unit(i):
        return plan[i][0] if i + 1 == TILES or plan[i + 1][0] != plan[i][0] else None

    def hf_slot(unit):
        return 1 if unit == HU else unit % 2

    def flag(i):
        return ps_s[0:1, i % 2, 0:1]

    def quads(eng, body, lag):
        for i in range(TILES):
            body(0, i, True)
        with eng.Fori(1, NQ) as q:
            for i in range(TILES):
                body(q, i, False)
        if lag:
            for i in range(lag):
                body(NQ, i, False)

    with nc.Block() as block:

        @block.sync
        def _(sp):
            def load_qk(b, hq, slot):
                h = HQ * hq
                for r, (a, c) in enumerate(PAIRS):
                    for dst, src, s in ((q_sb, q_parts, a), (k_sb, k_parts, c)):
                        sp.dma_start(dst[D * r:D * (r + 1), slot, :, :],
                                     src[b, s, h * D:(h + HQ) * D, :].rearrange("(j d) t -> d j t", d=D))\
                          .then_inc(qk_in, 16)
                sp.dma_start(q_sb[QROWS:K_ROWS, slot, :, :],
                             far_q[:, :, h:h + HQ, :].rearrange("s r j t -> (s r) j t")).then_inc(qk_in, 16)

            def load_band(hq):
                sp.dma_start(band[:, :, :, :].rearrange("p j s c -> p j (s c)"),
                             toep[HQ * hq:HQ * (hq + 1)].rearrange("h p c -> p h c")).then_inc(band_in, 16)

            def load_xp(b, hq):
                sp.dma_start(xp[:, :, :, :], x_parts[b, :, :, :, FT * hq:FT * (hq + 1)]).then_inc(xp_in, 16)

            def load_v(b, hq):
                sp.dma_start(v_next[:, :, :, :].rearrange("p j k d -> p (j k d)"),
                             v_all[b, :, HQ * hq:HQ * (hq + 1)].rearrange("p j k d -> p (j k d)"))\
                  .then_inc(v_in, 16)

            def load_acc(b, slot):
                sp.dma_start(acc[:, slot, :, :], out[b].rearrange("(t p) e -> p t e", p=P)).then_inc(acc_in, 16)

            def store_acc(n, b, slot):
                hold(sp, acc_y, KB * (n + 1))
                hold(sp, acc_f, n + 1)
                sp.dma_start(out[b].rearrange("(t p) e -> p t e", p=P), acc[:, slot, :, :]).then_inc(out_sent, 16)
                hold(sp, out_sent, 16 * (n + 1))

            load_band(0)
            for s in range(3):
                sp.dma_start(k_sb[QROWS + KB * s:QROWS + KB * (s + 1), :, :, :].rearrange("r a j t -> r (a j) t"),
                             block_of_key.unsqueeze(1).broadcast_to([KB, 2 * HQ, T])).then_inc(once_in, 16)
            load_qk(0, 0, 0)
            load_xp(0, 0)
            load_v(0, 0)
            load_acc(0, 0)

            def quad(hq, b, new_heads, last_of_heads):
                n = hq * B + b
                first, last = hq == 0 and new_heads, hq == QUADS - 1 and last_of_heads
                nb, nh, slot = (0, hq + 1, B % 2) if last_of_heads else (b + 1, hq, (b + 1) % 2)
                if not first:
                    hold(sp, s_ready, n * TILES)
                    if new_heads:
                        load_band(hq)
                if not last:
                    hold(sp, qk_in, QK_IN * (n + 1))
                    load_qk(nb, nh, slot)
                    hold(sp, ffn_ready, n * UNITS + MT // 2)
                    load_xp(nb, nh)
                if not last:
                    hold(sp, v_ready, n + 1)
                    load_v(nb, nh)
                if not first:
                    store_acc(n - 1, B - 1 if new_heads else b - 1, (b + 1) % 2)
                if not last:
                    hold(sp, acc_in, 16 * (n + 1))
                    load_acc(nb, slot)

            for hq in range(QUADS):
                quad(hq, 0, True, False)
                with sp.Fori(1, B - 1) as b:
                    quad(hq, b, False, False)
                quad(hq, B - 1, False, True)
            store_acc(NQ - 1, B - 1, (NQ - 1) % 2)

        @block.tensor
        def _(pe):
            def scores(q, i):
                qi, j, slot = i // HQ, i % HQ, q % 2
                t = q * TILES + i
                ps = ps_s[:, i % 2, :]
                near = range(max(qi - 3, 0), min(qi + 2, KB))
                for half in range(2):
                    blocks = [k for k in near if k // 4 == half]
                    mm = pe.matmul(ps[:, half * 512:(half + 1) * 512],
                                   q_sb[0:K_ROWS, slot, j, qi * P:(qi + 1) * P],
                                   k_sb[0:K_ROWS, slot, j, half * 512:(half + 1) * 512],
                                   start=True, stop=not blocks)
                    for s in range(3 if blocks else 0):
                        c = (blocks[0] - qi + 3) * P
                        w = len(blocks) * P
                        mm = pe.matmul(ps[:, blocks[0] * P:blocks[0] * P + w], flip[:, :],
                                       band[:, j, s, c:c + w], start=False, stop=(s == 2))
                mm.then_inc(s_ready, 1)

            def feed_forward(q, first, unit, a, b, last):
                if a == 0 and not (first and unit == 0):
                    pe.wait_ge(ffn_taken, q * UNITS + unit)
                if unit == 0:
                    pe.wait_ge(xp_in, 16 * (q + 1))
                for n in range(a, b):
                    k, s, u = n // PARTS, n % PARTS // 2, n % 2
                    if n % (2 * PARTS) == 0 and unit in (MT // 2, HU):
                        pe.wait_ge(h_ready, q * HU + (0 if unit < HU else MT // 2) + n // (2 * PARTS) + 1)
                    if unit < MT // 2:
                        m = 2 * unit + u
                        lhs, rhs = w0[:, k, m * P:(m + 1) * P], xp[:, k, s, :]
                    elif unit < HU:
                        m = 2 * (unit - MT // 2) + u
                        lhs, rhs = w1[:, k, m * P:(m + 1) * P], h0[:, k, s, :]
                    else:
                        lhs, rhs = h1[:, k, s, u * P:(u + 1) * P], w2[:, k, :]
                    mm = pe.matmul(ps_f[:, u, :], lhs, rhs, start=(n == 0), stop=(last and n >= b - 2),
                                   skip_group_check=True)
                if last:
                    mm.then_inc(ffn_ready, 1)

            def turn(t, i):
                for half in range(2):
                    if not (isinstance(t, int) and t == 0):
                        pe.wait_ge(pT_ready, 2 * t - 1 + half)
                    for k in range(4 * half, 4 * half + 4):
                        tr = pe.transpose(ps_t[:, half, (k % 4) * P:(k % 4 + 1) * P],
                                          e_sb[:, i % 4, k * P:(k + 1) * P], ident[:, :])
                    tr.then_inc(p_turned, 1)

            def body(q, i, first):
                t = q * TILES + i
                over = isinstance(q, int) and q == NQ
                if not over:
                    if i == 0:
                        if first:
                            pe.wait_ge(once_in, 48)
                        pe.wait_ge(qk_in, QK_IN * (q + 1))
                        pe.wait_ge(band_in, 16 * (q // B + 1))
                    if not (first and i < 4):
                        pe.wait_ge(hidden_in, t - 3)
                    elif i >= 2:
                        pe.wait_ge(s_taken, i - 1)
                    scores(q, i)
                if not (first and i < 5) and not (over and i >= 5):
                    pe.wait_ge(*masked(q, i - 5))
                    turn(t - 5, i - 5)
                if not (first and i < 3) and not (over and i >= 3):
                    if first and i == 3:
                        pe.wait_ge(ones_ready, 1)
                    pe.wait_ge(hides_ready, t - 2)
                    if not over or i == 0:
                        pe.wait_ge(s_taken, t)
                    elif i == 2:
                        pe.wait_ge(hidden_in, t - 4)
                    pe.matmul(flag(i - 3), hides[:, (i - 3) % 2:(i - 3) % 2 + 1], ones[:, :],
                              start=True, stop=True).then_inc(hidden_ready, 1)
                if not (first and i < PV) and not (over and i >= PV):
                    step = (i - PV) % HQ
                    m = in_group(q, i, PV + step)
                    mp = (i - PV) // HQ % 2
                    if step == 0:
                        if first and i == PV:
                            pe.wait_ge(o_cleared, 1)
                        else:
                            pe.wait_ge(pv_taken, m)
                        if i == PV:
                            pe.wait_ge(v_ready, q + 1)
                        pe.wait_ge(pT_ready, 2 * HQ * (m + 1))
                    if step == (OUT - PV) % HQ + 1 and not (first and i < PV + HQ):
                        pe.wait_ge(y_taken, m)
                    for k in range(KB // HQ * step, KB // HQ * (step + 1)):
                        for j in range(HQ):
                            mm = pe.matmul(ps_o[PD * j:PD * j + D, 0:P], v_sb[:, j, k, :], pT[:, mp, j, k, :],
                                           start=(k == 0), stop=(k == KB - 1), skip_group_check=True)
                    if step == HQ - 1:
                        pe.wait_ge(rwide_ready, m + 1)
                        mm = pe.transpose(ps_o[:, P:2 * P], rwide[:, :, :].rearrange("p j d -> p (j d)"),
                                          ident[:, :])
                        mm.then_inc(pv_ready, 1)
                m = in_group(q, i, OUT)
                if m is not None and not (first and i < OUT):
                    hq = q // B if i >= OUT else (q - 1) // B
                    pe.wait_ge(attn_ready, m + 1)
                    alone = over and i + HQ >= OUT
                    if alone:
                        pe.wait_ge(y_taken, m)
                    pe.matmul(ps_o[:, yc:yc + C], attnT[:, (i - OUT) // HQ % 2, :], woT[:, hq, :],
                              start=alone, stop=True, skip_group_check=True).then_inc(y_ready, 1)
                if not over:
                    feed_forward(q, first, *plan[i], ended_unit(i) is not None)

            quads(pe, body, OUT - HQ + 1)

        @block.scalar
        def _(act):
            def body(q, i, first):
                t = q * TILES + i
                over = isinstance(q, int) and q == NQ
                if not over:
                    act.wait_ge(s_ready, t + 1)
                    if not (first and i < 4):
                        act.wait_ge(*((kept_step, halves(q, i - 4) + 1) if i % 2 else masked(q, i - 4)))
                    act.activation(s_sb[:, i % 4, :], ps_s[:, i % 2, :], ACT.Copy).then_inc(s_taken, 1)
                if not (first and i < 2) and not (over and i >= 2):
                    act.wait_ge(neg_ready, t - 1)
                    if not (first and i < 6):
                        act.wait_ge(p_turned, 2 * (t - 5))
                    if i % 2 and not (first and i < 7):
                        act.wait_ge(summed, halves(q, i - 6) + 1)
                    act.activation(e_sb[:, (i - 2) % 4, :], s_sb[:, (i - 2) % 4, :], ACT.Exp,
                                   bias=neg_max[:, (i - 2) % 4:(i - 2) % 4 + 1]).then_inc(e_ready, 1)
                unit = ended_unit(i)
                if unit is not None and not over:
                    act.wait_ge(ffn_ready, q * UNITS + unit + 1)
                    if unit == HU:
                        act.wait_ge(h_ready, q * HU + HU)
                    elif unit >= 2:
                        act.wait_ge(h_ready, q * HU + unit - 1)
                    elif not first:
                        act.wait_ge(*((h_ready, q * HU - 1), (acc_f, q))[unit])
                    layer = 2 if unit == HU else unit // (MT // 2)
                    ins = act.activation(hf[:, hf_slot(unit), :, :], ps_f[:, :, :],
                                         ACT.Identity if layer == 2 else ACT.Relu,
                                         scale=scales[:, layer:layer + 1])
                    if unit < HU:
                        u = unit % (MT // 2)
                        ins = act.activation((h0, h1)[layer][:, 2 * u:2 * u + 2, 0, :], ps_f[:, :, :], ACT.Relu,
                                             scale=scales[:, layer:layer + 1])
                    ins.then_inc(ffn_taken, 1)
                if i == PV - 1 and not over:
                    act.wait_ge(v_in, 16 * (q + 1))
                    if not first:
                        act.wait_ge(pv_ready, q * KB)
                    act.activation(v_sb[:, :, :, :], v_next[:, :, :, :], ACT.Copy).then_inc(v_ready, 1)
                if not (first and i < 4) and not (over and i >= 4):
                    mp, j = ((i - 4) // HQ) % 2, i % HQ
                    if not (first and i < 12):
                        act.wait_ge(pv_ready, q * KB + (i - 12) // HQ + 1)
                    for half in range(2):
                        act.wait_ge(p_turned, 2 * (t - 4) + 1 + half)
                        act.activation(pT[:, mp, j, 4 * half:4 * half + 4, :], ps_t[:, half, :], ACT.Copy)\
                           .then_inc(pT_ready, 1)
                if not (first and i < 2) and not (over and i >= 2):
                    act.wait_ge(hidden_ready, t - 1)
                    act.activation(hidden_sb[:, (i - 2) % 4:(i - 2) % 4 + 1], flag(i - 2), ACT.Copy)\
                       .then_inc(hidden_in, 1)
                m = in_group(q, i, PV_COPY)
                if m is not None and not (first and i < PV_COPY):
                    act.wait_ge(pv_ready, m + 1)
                    if not (first and i == PV_COPY):
                        act.wait_ge(attn_ready, m)
                    act.activation(orT[:, :, :], ps_o[:, 0:2 * P], ACT.Copy).then_inc(pv_taken, 1)
                m = in_group(q, i, OUT_COPY)
                if m is not None and not (first and i < OUT_COPY):
                    act.wait_ge(y_ready, m + 1)
                    if not (first and i < OUT_COPY + 2 * HQ):
                        act.wait_ge(acc_y, m - 1)
                    act.activation(y[:, (i - OUT_COPY) // HQ % 2, :], ps_o[:, yc:yc + C], ACT.Copy)\
                       .then_inc(y_taken, 1)
                if i % 2 == 0 and not (first and i < 6) and not (over and i >= 5):
                    n = i - 5
                    act.wait_ge(p_pool, halves(q, n) + 1)
                    if not (first and i < 14):
                        act.wait_ge(rden_ready, q * KB + n // HQ - 1)
                    act.activation(kept[:, n % HQ // 2, :], e_sb[:, n % 4, :], ACT.Copy,
                                   accum_out=den[:, n // HQ % 2, n % HQ:n % HQ + 1]).then_inc(summed, 1)

            quads(act, body, OUT_COPY - HQ + 1)

        @block.gpsimd
        def _(pool):
            pool.memset(ones[:, :], 1.0).then_inc(ones_ready, 1)

            def body(q, i, first):
                t = q * TILES + i
                over = isinstance(q, int) and q == NQ
                n = i - 2
                masks = n % 2 == 1 and not (first and n < 0) and not (over and n >= 0)
                if masks:
                    hold(pool, checked, halves(q, n) + 1)
                    if not (first and n < 4):
                        hold(pool, summed, halves(q, n) - 1)
                    pool.tensor_scalar(kept[:, n % HQ // 2, :], s_sb[:, n % 4, :], top[:, n % 4, TOPK - 1:TOPK],
                                       None, ALU.is_ge).then_inc(kept_step, 1)
                if not over:
                    hold(pool, max_ready, t + 1)
                    if not (first and i < 4):
                        hold(pool, e_ready, t - 3)
                    pool.tensor_scalar(neg_max[:, i % 4:i % 4 + 1], top[:, i % 4, 0:1], -1.0, None, ALU.mult)\
                        .then_inc(neg_ready, 1)
                if masks:
                    hold(pool, e_ready, t - 1)
                    hold(pool, kept_step, halves(q, n) + 1)
                    e = e_sb[:, n % 4, :]
                    pool.tensor_tensor(e, e, kept[:, n % HQ // 2, :], ALU.mult).then_inc(p_pool, 1)
                m = in_group(q, i, RWIDE)
                if m is not None and not (first and i < RWIDE) and not (over and i >= RWIDE):
                    hold(pool, rden_ready, m + 1)
                    if not (first and i == RWIDE):
                        hold(pool, pv_ready, m)
                    pool.tensor_copy(rwide[:, :, :],
                                     rden[:, (i - RWIDE) // HQ % 2, :].unsqueeze(2).broadcast_to([P, HQ, PD]))\
                        .then_inc(rwide_ready, 1)
                m = in_group(q, i, PV_COPY)
                if m is not None and not (first and i < PV_COPY) and not (over and i >= PV_COPY):
                    hold(pool, pv_taken, m + 1)
                    if not (first and i < PV_COPY + 2 * HQ):
                        hold(pool, y_ready, m - 1)
                    pool.tensor_tensor(attnT[:, (i - PV_COPY) // HQ % 2, :], orT[:, 0, :], orT[:, 1, :], ALU.mult)\
                        .then_inc(attn_ready, 1)
                m = in_group(q, i, OUT_ADD)
                if m is not None and not (first and i < OUT_ADD):
                    tile = (i - OUT_ADD) // HQ
                    if tile == 0:
                        hold(pool, acc_in, 16 * (q + 1))
                    if i == OUT_ADD % HQ:
                        hold(pool, acc_f, q)
                    hold(pool, y_taken, m + 1)
                    a = acc[:, (q if tile >= 0 else q + 1) % 2, tile % KB, :]
                    pool.tensor_tensor(a, a, y[:, tile % 2, :], ALU.add).then_inc(acc_y, 1)
                unit = ended_unit(i)
                if unit is not None and not over:
                    hold(pool, ffn_taken, q * UNITS + unit + 1)
                    src = hf[:, hf_slot(unit), :, :]
                    if unit < HU:
                        u = unit % (MT // 2)
                        parts = [(h0, h1)[unit // (MT // 2)][:, 2 * u:2 * u + 2, s, :] for s in range(3)]
                        pool.tensor_tensor(parts[1], src, parts[0], ALU.subtract)
                        pool.tensor_tensor(src, src, parts[0], ALU.subtract).then_inc(split_step, 1)
                        pool.wait_ge(split_step, 1)
                        pool.sem_inc(split_step, -1)
                        pool.tensor_tensor(parts[2], src, parts[1], ALU.subtract).then_inc(h_ready, 1)
                    else:
                        hold(pool, acc_y, q * KB + (TILES - 1 - OUT_ADD) // HQ + 1)
                        a = acc[:, :, :, :].rearrange("p s (g u) e -> p s g u e", u=2)[:, q % 2, q // B, :, :]
                        pool.tensor_tensor(a, a, src, ALU.add).then_inc(acc_f, 1)

            quads(pool, body, OUT_ADD - HQ + 1)

        @block.vector
        def _(dve):
            CHAIN = 2 * (TOPK // 8) - 1

            def part_of(s, c):
                n = (T // 4 - c + CHUNKS - 1) // CHUNKS
                return bass.AP(tensor=s.tensor, offset=s.offset + 4 * c, ap=[s.ap[0], [4 * CHUNKS, n], [1, 4]])

            def ranks(i, a, b):
                return cand[:, i % 2, 8 + (a - 1) * CHUNKS:8 + b * CHUNKS].rearrange("p (r c) -> p r c", c=CHUNKS)

            def exact(i):
                s, tp, w = s_sb[:, i % 4, :], top[:, i % 4, :], work[:, :]
                for n in range(1, TOPK // 8):
                    dve.match_replace(w, tp[:, 8 * n - 8:8 * n], s if n == 1 else w, NEG).then_inc(exact_step, 1)
                    dve.wait_ge(exact_step, 2 * n - 1)
                    dve.max(tp[:, 8 * n:8 * n + 8], w).then_inc(exact_step, 1)
                    if n < TOPK // 8 - 1:
                        dve.wait_ge(exact_step, 2 * n)
                dve.wait_ge(exact_step, CHAIN - 1)
                dve.sem_inc(exact_step, 1 - CHAIN)

            def body(q, i, first):
                t = q * TILES + i
                over = isinstance(q, int) and q == NQ
                chunks = iter([] if over else range(CHUNKS))
                picks = not (first and i < 1) and not (over and i >= 1)
                masks = not (first and i < 2) and not (over and i >= 2)
                m = in_group(q, i, RDEN)

                def fill(n):
                    for _ in range(n):
                        c = next(chunks, None)
                        if c is not None:
                            ins = dve.max(ranks(i, 1, 8)[:, :, c], part_of(s_sb[:, i % 4, :], c))
                            if c == 3 and picks:
                                ins.then_inc(max_ready, 1)
                            if c == CHUNKS - 1:
                                ins.then_inc(cand_ready, 1)

                if not over:
                    hold(dve, s_taken, t + 1)
                if picks:
                    tp = top[:, (i - 1) % 4, :]
                    src = cand[:, (i - 1) % 2, 0:8 + 3 * CHUNKS]
                    deep = cand[:, (i - 1) % 2, 0:8]
                    dve.wait_ge(cand_ready, 1)
                    dve.sem_inc(cand_ready, -1)
                    dve.max(deep, ranks(i - 1, 4, 7)).then_inc(top_step, 1)
                    fill(3)
                    dve.wait_ge(top_step, 1)
                    dve.max(tp[:, 0:8], src).then_inc(top_step, 1)
                    if over:
                        dve.wait_ge(top_step, 2)
                        dve.sem_inc(max_ready, 1)
                    else:
                        fill(3)
                    for n in range(1, TOPK // 8):
                        dve.wait_ge(top_step, 2 * n)
                        dve.match_replace(rest[:, :], tp[:, 8 * n - 8:8 * n], src if n == 1 else rest[:, :], NEG)\
                           .then_inc(top_step, 1)
                        fill(3)
                        dve.wait_ge(top_step, 2 * n + 1)
                        dve.max(tp[:, 8 * n:8 * n + 8], rest[:, :]).then_inc(top_step, 1)
                        fill(3 if n < TOPK // 8 - 1 else 0)
                    dve.tensor_scalar(eighth[:, :], ranks(i - 1, 8, 8), deep[:, 7:8], None, ALU.max, ALU.max,
                                      accum_out=unseen[:, (i - 1) % 2:(i - 1) % 2 + 1]).then_inc(top_step, 1)
                if m is not None and not (first and i < RDEN):
                    if over:
                        dve.wait_ge(*masked(q, i - 7))
                        dve.wait_ge(summed, 2 * (m + 1))
                    mp = (i - RDEN) // HQ % 2
                    dve.reciprocal(rden[:, mp, :], den[:, mp, :]).then_inc(rden_ready, 1)
                fill(CHUNKS)
                if masks:
                    if i % 2 == 0:
                        dve.wait_ge(e_ready, t - 1)
                    hold(dve, hidden_in, t - 1)
                    hidden = dve.value_load(hidden_sb[0:1, (i - 2) % 4:(i - 2) % 4 + 1].bitcast(mybir.dt.int32))
                    with dve.If(hidden != 0):
                        exact(i - 2)
                    if i % 2:
                        dve.sem_inc(checked, 1)
                if picks:
                    dve.wait_ge(top_step, CHAIN + 2)
                    dve.sem_inc(top_step, -(CHAIN + 2))
                    dve.tensor_tensor(hides[:, (i - 1) % 2:(i - 1) % 2 + 1], unseen[:, (i - 1) % 2:(i - 1) % 2 + 1],
                                      tp[:, TOPK - 1:TOPK], ALU.is_gt).then_inc(hides_ready, 1)
                if masks:
                    mp, j = ((i - 2) // HQ) % 2, (i - 2) % HQ
                    if i % 2 == 0:
                        e, s = e_sb[:, (i - 2) % 4, :], s_sb[:, (i - 2) % 4, :]
                        dve.scalar_tensor_tensor(out=e, in0=s, scalar=top[:, (i - 2) % 4, TOPK - 1:TOPK], in1=e,
                                                 op0=ALU.is_ge, op1=ALU.mult, accum_out=den[:, mp, j:j + 1])\
                           .then_inc(p_dve, 1)

            dve.memset(ps_o[:, 0:P], 0.0).then_inc(o_cleared, 1)
            quads(dve, body, RDEN - HQ + 1)


_INS = ["L0_attn_x", "L0_attn_Wq", "L0_attn_bq", "L0_attn_Wk", "L0_attn_bk", "L0_attn_Wv", "L0_attn_bv",
        "L0_attn_Wo", "L0_attn_bo", "L0_attn_head_gates", "L0_attn_rel_bias", "L0_ffn_k0", "L0_ffn_k1",
        "L0_ffn_k2", "L0_ffn_s0", "L0_ffn_s1", "L0_ffn_s2"]


def kernel(**inputs):
    import numpy as _np
    import concourse.bacc as _bacc
    from concourse import mybir as _mybir
    from concourse.bass_utils import run_bass_kernel_spmd as _run

    nc = _bacc.Bacc("TRN2", target_bir_lowering=False, num_devices=1)
    arrays, args = {}, []
    for name in _INS:
        a = _np.ascontiguousarray(inputs[name])
        a = a.reshape(a.shape or (1,))
        arrays[f"in_{name}_dram"] = a
        args.append(nc.dram_tensor(f"in_{name}_dram", a.shape, _mybir.dt.from_np(a.dtype), kind="ExternalInput").ap())
    out = nc.dram_tensor("out_0_dram", inputs["L0_attn_x"].shape, F32, kind="ExternalOutput").ap()
    attention_ffn_kernel(nc, *args, out)
    r = _run(nc, [arrays], core_ids=[0])
    return r.results[0]["out_0_dram"]
```
